# Optimizing a Trainium2 kernel written in Bass

```python
import numpy as np
import jax
import jax.numpy as jnp

def _softmax(x, axis=-1):
    return jax.nn.softmax(x, axis=axis)

def _gelu(x):
    return jax.nn.gelu(x, approximate=True)

def _silu(x):
    return jax.nn.silu(x)

def _sigmoid(x):
    return jax.nn.sigmoid(x)

def _layernorm(x, axis=-1, eps=1e-05):
    m = jnp.mean(x, axis=axis, keepdims=True)
    v = jnp.var(x, axis=axis, keepdims=True)
    return (x - m) / jnp.sqrt(v + eps)

def _scatter_add(tgt, idx, src, axis=0):
    return tgt.at[idx].add(src)

def _segment_sum(src, seg, n):
    return jax.ops.segment_sum(src, seg, n)
kernel_name = 'mk_seq_preln_d1_jaxref_r8_21e71d'

def setup_inputs(seed: int=0):
    np.random.seed(seed)
    _w = jnp.asarray

    def _L0_attn_setup():
        import jax, jax.numpy as jnp
        import numpy as np
        H = 512
        D_IN = 1024
        N = 16
        K = 4
        R = 32
        EPS = 1e-06

        def rms_forward(x, eps=EPS):
            xf = x.astype(jnp.float32)
            var = jnp.mean(xf * xf, axis=-1, keepdims=True)
            return (xf * jax.lax.rsqrt(var + eps)).astype(x.dtype)
        key = jax.random.key(seed)
        ks = jax.random.split(key, 10)
        s = 0.02
        hidden_states = jax.random.normal(ks[0], (2, 128, H), dtype=jnp.float32)
        W_in = jax.random.normal(ks[1], (2 * D_IN, H), dtype=jnp.float32) * s
        conv_w = jax.random.normal(ks[2], (D_IN, K), dtype=jnp.float32) * 0.2
        conv_b = jax.random.normal(ks[3], (D_IN,), dtype=jnp.float32) * 0.02
        W_x = jax.random.normal(ks[4], (R + 2 * N, D_IN), dtype=jnp.float32) * s
        W_dt = jax.random.normal(ks[5], (D_IN, R), dtype=jnp.float32) * s
        b_dt = jax.random.normal(ks[6], (D_IN,), dtype=jnp.float32) * 0.02
        A_log = jnp.log(jnp.broadcast_to(jnp.arange(1, N + 1, dtype=jnp.float32)[None, :], (D_IN, N)))
        D = jnp.ones((D_IN,), dtype=jnp.float32)
        W_out = jax.random.normal(ks[7], (H, D_IN), dtype=jnp.float32) * s
        return {'hidden_states': hidden_states, 'W_in': W_in, 'conv_w': conv_w, 'conv_b': conv_b, 'W_x': W_x, 'W_dt': W_dt, 'b_dt': b_dt, 'A_log': A_log, 'D': D, 'W_out': W_out}
    _L0_attn_in = _L0_attn_setup()

    def _L0_ffn_setup():
        import jax, jax.numpy as jnp
        import numpy as np
        HIDDEN = 512
        INTER = 1376
        GROUP = 128
        B, S = (4, 256)
        NIB = jnp.uint32(15)

        def _pack_rows(nib):
            r = nib.reshape(-1, 8, nib.shape[-1])
            shifts = (jnp.arange(8, dtype=jnp.uint32) * 4)[None, :, None]
            return jnp.sum(r << shifts, axis=1, dtype=jnp.uint32)

        def _pack_cols(nib):
            r = nib.reshape(nib.shape[0], -1, 8)
            shifts = (jnp.arange(8, dtype=jnp.uint32) * 4)[None, None, :]
            return jnp.sum(r << shifts, axis=2, dtype=jnp.uint32)

        def _dequant(qw, qz, sc, g_idx):
            shifts = jnp.arange(8, dtype=jnp.uint32) * 4
            wq = qw[:, None, :] >> shifts[None, :, None] & NIB
            wq = wq.reshape(-1, qw.shape[1]).astype(jnp.float32)
            zq = qz[:, :, None] >> shifts[None, None, :] & NIB
            zq = zq.reshape(qz.shape[0], -1).astype(jnp.float32) + 1.0
            return sc[g_idx] * (wq - zq[g_idx])
        key = jax.random.key(seed)
        ks = jax.random.split(key, 7)
        n_groups = HIDDEN // GROUP
        n_groups_d = INTER // GROUP
        x = jax.random.normal(ks[0], (B, S, HIDDEN), jnp.float32)
        nib_w_gu = jax.random.randint(ks[1], (HIDDEN, 2 * INTER), 0, 16).astype(jnp.uint32)
        nib_z_gu = jax.random.randint(ks[2], (n_groups, 2 * INTER), 0, 15).astype(jnp.uint32)
        qweight_gu = _pack_rows(nib_w_gu)
        qzeros_gu = _pack_cols(nib_z_gu)
        scales_gu = jax.random.uniform(ks[3], (n_groups, 2 * INTER), jnp.float32, 0.005, 0.02)
        g_idx_gu = jnp.arange(HIDDEN, dtype=jnp.int32) // GROUP
        nib_w_d = jax.random.randint(ks[4], (INTER, HIDDEN), 0, 16).astype(jnp.uint32)
        nib_z_d = jax.random.randint(ks[5], (n_groups_d, HIDDEN), 0, 15).astype(jnp.uint32)
        qweight_down = _pack_rows(nib_w_d)
        qzeros_down = _pack_cols(nib_z_d)
        scales_down = jax.random.uniform(ks[6], (n_groups_d, HIDDEN), jnp.float32, 0.005, 0.02)
        g_idx_down = jnp.arange(INTER, dtype=jnp.int32) // GROUP
        return {'x': x, 'qweight_gu': qweight_gu, 'qzeros_gu': qzeros_gu, 'scales_gu': scales_gu, 'g_idx_gu': g_idx_gu, 'qweight_down': qweight_down, 'qzeros_down': qzeros_down, 'scales_down': scales_down, 'g_idx_down': g_idx_down}
    _L0_ffn_in = _L0_ffn_setup()
    _d = {'L0_attn_hidden_states': _L0_attn_in['hidden_states'], 'L0_attn_W_in': _L0_attn_in['W_in'], 'L0_attn_conv_w': _L0_attn_in['conv_w'], 'L0_attn_conv_b': _L0_attn_in['conv_b'], 'L0_attn_W_x': _L0_attn_in['W_x'], 'L0_attn_W_dt': _L0_attn_in['W_dt'], 'L0_attn_b_dt': _L0_attn_in['b_dt'], 'L0_attn_A_log': _L0_attn_in['A_log'], 'L0_attn_D': _L0_attn_in['D'], 'L0_attn_W_out': _L0_attn_in['W_out'], 'L0_ffn_qweight_gu': _L0_ffn_in['qweight_gu'], 'L0_ffn_qzeros_gu': _L0_ffn_in['qzeros_gu'], 'L0_ffn_scales_gu': _L0_ffn_in['scales_gu'], 'L0_ffn_g_idx_gu': _L0_ffn_in['g_idx_gu'], 'L0_ffn_qweight_down': _L0_ffn_in['qweight_down'], 'L0_ffn_qzeros_down': _L0_ffn_in['qzeros_down'], 'L0_ffn_scales_down': _L0_ffn_in['scales_down'], 'L0_ffn_g_idx_down': _L0_ffn_in['g_idx_down']}
    _x0 = _d['L0_attn_hidden_states']
    _d['L0_attn_hidden_states'] = jax.random.normal(jax.random.fold_in(jax.random.key(seed), 1), (4, 512, 512), dtype=_x0.dtype)
    del _x0
    return _d

def reference(L0_attn_hidden_states, L0_attn_W_in, L0_attn_conv_w, L0_attn_conv_b, L0_attn_W_x, L0_attn_W_dt, L0_attn_b_dt, L0_attn_A_log, L0_attn_D, L0_attn_W_out, L0_ffn_qweight_gu, L0_ffn_qzeros_gu, L0_ffn_scales_gu, L0_ffn_g_idx_gu, L0_ffn_qweight_down, L0_ffn_qzeros_down, L0_ffn_scales_down, L0_ffn_g_idx_down):

    def _L0_attn_ref(hidden_states, W_in, conv_w, conv_b, W_x, W_dt, b_dt, A_log, D, W_out):
        import jax, jax.numpy as jnp
        import numpy as np
        H = 512
        D_IN = 1024
        N = 16
        K = 4
        R = 32
        EPS = 1e-06

        def rms_forward(x, eps=EPS):
            xf = x.astype(jnp.float32)
            var = jnp.mean(xf * xf, axis=-1, keepdims=True)
            return (xf * jax.lax.rsqrt(var + eps)).astype(x.dtype)
        b, L, _ = hidden_states.shape
        proj = hidden_states @ W_in.T
        x, gate = (proj[..., :D_IN], proj[..., D_IN:])
        xpad = jnp.pad(x, ((0, 0), (K - 1, 0), (0, 0)))
        xc = conv_b
        for j in range(K):
            xc = xc + conv_w[:, j] * xpad[:, j:j + L, :]
        x = jax.nn.silu(xc)
        ssm = x @ W_x.T
        ts, Bm, Cm = (ssm[..., :R], ssm[..., R:R + N], ssm[..., R + N:])
        ts = rms_forward(ts)
        Bm = rms_forward(Bm)
        Cm = rms_forward(Cm)
        dt = jax.nn.softplus(ts @ W_dt.T + b_dt)
        A = -jnp.exp(A_log.astype(jnp.float32))

        def step(state, inp):
            dt_t, B_t, C_t, u_t = inp
            dA = jnp.exp(dt_t[..., None] * A)
            state = state * dA + (dt_t * u_t)[..., None] * B_t[:, None, :]
            y = jnp.einsum('bdn,bn->bd', state, C_t)
            return (state, y)
        init = jnp.zeros((b, D_IN, N), dtype=jnp.float32)
        xs = (dt.transpose(1, 0, 2), Bm.transpose(1, 0, 2), Cm.transpose(1, 0, 2), x.transpose(1, 0, 2))
        _, ys = jax.lax.scan(step, init, xs)
        y = ys.transpose(1, 0, 2) + x * D
        y = y * jax.nn.silu(gate)
        return y @ W_out.T

    def _L0_ffn_ref(x, qweight_gu, qzeros_gu, scales_gu, g_idx_gu, qweight_down, qzeros_down, scales_down, g_idx_down):
        import jax, jax.numpy as jnp
        import numpy as np
        HIDDEN = 512
        INTER = 1376
        GROUP = 128
        B, S = (4, 256)
        NIB = jnp.uint32(15)

        def _pack_rows(nib):
            r = nib.reshape(-1, 8, nib.shape[-1])
            shifts = (jnp.arange(8, dtype=jnp.uint32) * 4)[None, :, None]
            return jnp.sum(r << shifts, axis=1, dtype=jnp.uint32)

        def _pack_cols(nib):
            r = nib.reshape(nib.shape[0], -1, 8)
            shifts = (jnp.arange(8, dtype=jnp.uint32) * 4)[None, None, :]
            return jnp.sum(r << shifts, axis=2, dtype=jnp.uint32)

        def _dequant(qw, qz, sc, g_idx):
            shifts = jnp.arange(8, dtype=jnp.uint32) * 4
            wq = qw[:, None, :] >> shifts[None, :, None] & NIB
            wq = wq.reshape(-1, qw.shape[1]).astype(jnp.float32)
            zq = qz[:, :, None] >> shifts[None, None, :] & NIB
            zq = zq.reshape(qz.shape[0], -1).astype(jnp.float32) + 1.0
            return sc[g_idx] * (wq - zq[g_idx])
        w_gu = _dequant(qweight_gu, qzeros_gu, scales_gu, g_idx_gu)
        inter = jnp.einsum('bsh,hf->bsf', x, w_gu)
        gate, up = (inter[..., :INTER], inter[..., INTER:])
        h = jax.nn.silu(gate) * up
        w_d = _dequant(qweight_down, qzeros_down, scales_down, g_idx_down)
        return jnp.einsum('bsf,fh->bsh', h, w_d)
    x = L0_attn_hidden_states
    x = x + _L0_attn_ref(_layernorm(x, axis=-1), L0_attn_W_in, L0_attn_conv_w, L0_attn_conv_b, L0_attn_W_x, L0_attn_W_dt, L0_attn_b_dt, L0_attn_A_log, L0_attn_D, L0_attn_W_out)
    x = x + _L0_ffn_ref(_layernorm(x, axis=-1), L0_ffn_qweight_gu, L0_ffn_qzeros_gu, L0_ffn_scales_gu, L0_ffn_g_idx_gu, L0_ffn_qweight_down, L0_ffn_qzeros_down, L0_ffn_scales_down, L0_ffn_g_idx_down)
    return x

_drawn_inputs = setup_inputs


def setup_inputs(seed=0):
    import zlib

    import numpy as np

    out = dict(_drawn_inputs(seed))
    spreads = {'L0_attn_D': (1.0, 0.6)}
    factors = {'L0_attn_conv_b': 4.461,
     'L0_attn_W_dt': 8.0,
     'L0_attn_b_dt': 43.104,
     'L0_attn_A_log': 14.377}
    for name, (base, spread) in spreads.items():
        noise = np.random.default_rng([zlib.crc32(name.encode()), seed]).standard_normal(out[name].shape)
        drawn = base * np.exp(spread * noise) if base else spread * noise
        out[name] = jnp.asarray(drawn.astype(out[name].dtype))
    for name, factor in factors.items():
        out[name] = (out[name] * factor).astype(out[name].dtype)
    return out
```

```python
from contextlib import ExitStack

import concourse.bass as bass
from concourse import mybir

F32 = mybir.dt.float32
F32R = mybir.dt.float32r
U32 = mybir.dt.uint32
I32 = mybir.dt.int32
ALU = mybir.AluOpType
ACT = mybir.ActivationFunctionType

P = 128
NB, L, H = 4, 512, 512
DI, NS, R = 1024, 16, 32
TB = L // P
KH = H // P
DT = DI // P
SF = R + 2 * NS
TAPS = 4
INTER = 1376
FT = -(-INTER // P)
FL = INTER - (FT - 1) * P
GRP = 128
NG, NGD = H // GRP, INTER // GRP
LN_EPS, RMS_EPS = 1e-5, 1e-6
QC = 8


def rows(ft):
    return P if ft < FT - 1 else FL


def products(pe, out, hi_l, lo_l, hi_r, lo_r, start, stop, **kw):
    pe.matmul(out, hi_l, hi_r, start=start, stop=False, **kw)
    pe.matmul(out, hi_l, lo_r, start=False, stop=False, **kw)
    return pe.matmul(out, lo_l, hi_r, start=False, stop=stop, **kw)


def layer_stats(dve, xall, stats, mv, var_e, st_done, mv_done, ve_done):
    for t in range(NB * TB):
        dve.bn_stats(stats[:, t, :], xall[:, t, :]).then_inc(st_done, 1)
    for t in range(NB * TB):
        dve.wait_ge(st_done, t + 1)
        dve.bn_aggr(mv[:, t, :], stats[:, t, :]).then_inc(mv_done, 1)
    dve.wait_ge(mv_done, NB * TB)
    dve.tensor_scalar(var_e[:, :], mv[:, :, 1], LN_EPS, None, ALU.add).then_inc(ve_done, 1)


def build(nc, x, w_in, conv_w, conv_b, w_x, w_dt, a_log, d_skip, w_out,
          qw_gu, qz_gu, sc_gu, gi_gu, qw_d, qz_d, sc_d, gi_d, out):
    u_d = nc.dram_tensor("u_scratch", (NB, DT, P, L), F32, kind="Internal").ap()
    g_d = nc.dram_tensor("gate_scratch", (NB, DT, P, L), F32, kind="Internal").ap()
    bc_d = nc.dram_tensor("bc_scratch", (NB, 2 * NS, L), F32, kind="Internal").ap()
    ts_d = nc.dram_tensor("ts_scratch", (NB, R, 2, L), F32, kind="Internal").ap()

    whole = ExitStack()
    with whole:
        def tensors(ctx):
            def sb(name, shape, dt=F32):
                return ctx.enter_context(nc.sbuf_tensor(name, shape, dt))

            def ps(name, shape):
                return ctx.enter_context(nc.psum_tensor(name, shape, F32))

            def sem(name):
                return ctx.enter_context(nc.semaphore(name))
            return sb, ps, sem

        sb, ps, sem = tensors(whole)
        xall = sb("xall", [P, NB * TB, H])
        ident = sb("ident", [P, P])
        a_neg = sb("a_neg", [P, DT, NS])
        dsk = sb("dsk", [P, DT])
        cw = sb("cw", [P, DT, TAPS])
        cb = sb("cb", [P, DT])
        x_in = [sem(f"x_in{b}") for b in range(NB)]
        outer = ExitStack()
        sbo, _, _ = tensors(outer)
        with outer:
            wdt_hi, wdt_lo = sbo("wdt_hi", [R + 1, DI], F32R), sbo("wdt_lo", [R + 1, DI], F32R)
            ts_hl = sbo("ts_hl", [R + 1, 2, L], F32R)
            attention(nc, tensors, xall, ident, a_neg, dsk, cw, cb, x_in, wdt_hi, wdt_lo, ts_hl,
                      x, w_in, conv_w, conv_b, w_x, w_dt, a_log, d_skip, w_out, u_d, g_d, bc_d, ts_d)
        ffn(nc, tensors, xall, ident, qw_gu, qz_gu, sc_gu, gi_gu, qw_d, qz_d, sc_d, gi_d, out)


def attention(nc, tensors, xall, ident, a_neg, dsk, cw, cb, x_in, wdt_hi, wdt_lo, ts_hl,
              x, w_in, conv_w, conv_b, w_x, w_dt, a_log, d_skip, w_out, u_d, g_d, bc_d, ts_d):
    with ExitStack() as c:
        sb, ps, sem = tensors(c)
        win_hi, win_lo = sb("win_hi", [P, KH, 2 * DI], F32R), sb("win_lo", [P, KH, 2 * DI], F32R)
        wx_hi, wx_lo = sb("wx_hi", [P, DT, SF], F32R), sb("wx_lo", [P, DT, SF], F32R)
        prepare(nc, tensors, xall, ident, a_neg, dsk, cw, cb, x_in, wdt_hi, wdt_lo, ts_hl,
                win_hi, win_lo, wx_hi, wx_lo, x, w_in, conv_w, conv_b, w_x, w_dt, a_log, d_skip)
        project(nc, tensors, xall, ident, cw, cb, win_hi, win_lo, wx_hi, wx_lo, u_d, g_d, bc_d, ts_d)
    scan(nc, tensors, xall, ident, a_neg, dsk, wdt_hi, wdt_lo, ts_hl, w_out, u_d, g_d, bc_d, ts_d)


def prepare(nc, tensors, xall, ident, a_neg, dsk, cw, cb, x_in, wdt_hi, wdt_lo, ts_hl,
            win_hi, win_lo, wx_hi, wx_lo, x, w_in, conv_w, conv_b, w_x, w_dt, a_log, d_skip):
    with ExitStack() as c:
        sb, ps, sem = tensors(c)
        wraw = sb("wraw", [P, KH, 2 * DI])
        wxraw = sb("wxraw", [P, DT, SF])
        wdraw = sb("wdraw", [R + 1, DI])
        win_in = [sem(f"win_in{k}") for k in range(KH)]
        small_in = sem("small_in")
        win_split = sem("win_split")
        win_rest = sem("win_rest")
        wx_split = sem("wx_split")
        wx_rest = sem("wx_rest")
        a_exp = sem("a_exp")
        a_done = sem("a_done")
        id_zero, id_done = sem("id_zero"), sem("id_done")
        ones_done = sem("ones_done")
        with nc.Block() as block:
            @block.sync
            def _(sp):
                for k in range(KH):
                    sp.dma_start(wraw[:, k, :], w_in[:, k, :]).then_inc(win_in[k], 16)
                sp.dma_start(wxraw[:, :, :], w_x).then_inc(small_in, 16)
                sp.dma_start(wdraw[:, :], w_dt).then_inc(small_in, 16)
                sp.dma_start(a_neg[:, :, :], a_log).then_inc(small_in, 16)
                sp.dma_start(dsk[:, :], d_skip).then_inc(small_in, 16)
                sp.dma_start(cw[:, :, :], conv_w).then_inc(small_in, 16)
                sp.dma_start(cb[:, :], conv_b).then_inc(small_in, 16)
                for b in range(NB):
                    sp.dma_start(xall[:, TB * b:TB * (b + 1), :], x[b]).then_inc(x_in[b], 16)
                for b in range(NB):
                    sp.wait_ge(x_in[b], 16)

            @block.scalar
            def _(act):
                for k in range(KH):
                    act.wait_ge(win_in[k], 16)
                    act.activation(win_hi[:, k, :], wraw[:, k, :], ACT.Copy).then_inc(win_split, 1)
                act.wait_ge(small_in, 96)
                act.activation(wx_hi[:, :, :], wxraw[:, :, :], ACT.Copy).then_inc(wx_split, 1)
                act.activation(wdt_hi[:, :], wdraw[:, :], ACT.Copy).then_inc(wx_split, 1)
                act.activation(a_neg[:, :, :], a_neg[:, :, :], ACT.Exp).then_inc(a_exp, 1)

            @block.vector
            def _(dve):
                for k in range(0, KH):
                    dve.wait_ge(win_split, k + 1)
                    dve.tensor_tensor(win_lo[:, k, 0:DI + 512], wraw[:, k, 0:DI + 512],
                                      win_hi[:, k, 0:DI + 512].bitcast(F32), ALU.subtract).then_inc(win_rest, 1)
                dve.wait_ge(wx_split, 2)
                dve.tensor_tensor(wx_lo[:, :, :], wxraw[:, :, :], wx_hi[:, :, :].bitcast(F32),
                                  ALU.subtract).then_inc(wx_rest, 1)
                dve.tensor_tensor(wdt_lo[:, :], wdraw[:, :], wdt_hi[:, :].bitcast(F32),
                                  ALU.subtract).then_inc(wx_rest, 1)
                dve.memset(ts_hl[R:R + 1, 0, :].bitcast(F32), 1.0).then_inc(ones_done, 1)
                dve.memset(ts_hl[R:R + 1, 1, :].bitcast(F32), 0.0).then_inc(ones_done, 1)
                dve.wait_ge(a_exp, 1)
                dve.tensor_scalar(a_neg[:, :, :], a_neg[:, :, :], -1.0, None, ALU.mult).then_inc(a_done, 1)

            @block.gpsimd
            def _(pool):
                pool.memset(ident[:, :], 0.0).then_inc(id_zero, 1)
                pool.wait_ge(id_zero, 1)
                pool.affine_select(out=ident[:, :], in_=ident[:, :], compare_op=ALU.not_equal, fill=1.0,
                                   base=0, pattern=[[-1, P]], channel_multiplier=1).then_inc(id_done, 1)
                for k in range(0, KH):
                    pool.wait_ge(win_split, k + 1)
                    pool.tensor_tensor(win_lo[:, k, DI + 512:], wraw[:, k, DI + 512:],
                                       win_hi[:, k, DI + 512:].bitcast(F32), ALU.subtract)


def project(nc, tensors, xall, ident, cw, cb, win_hi, win_lo, wx_hi, wx_lo, u_d, g_d, bc_d, ts_d):
    NR = 3
    with ExitStack() as c:
        sb, ps, sem = tensors(c)
        stats = sb("stats", [P, NB * TB, 6])
        mv = sb("mv", [P, NB * TB, 2])
        var_e = sb("var_e", [P, NB * TB])
        std = sb("std", [P, NB * TB])
        rstd = sb("rstd", [P, NB * TB])
        xn = sb("xn", [P, TB, H])
        xt_hi, xt_lo = sb("xt_hi", [P, KH, L], F32R), sb("xt_lo", [P, KH, L], F32R)
        xc = sb("xc", [P, 2, L])
        u = sb("u", [P, 2, L])
        u_hi, u_lo = sb("u_hi", [P, 2, L], F32R), sb("u_lo", [P, 2, L], F32R)
        g = sb("g", [P, 2, L])
        feat = sb("feat", [P, TB, SF])
        fsq = sb("fsq", [P, SF])
        ms = sb("ms", [P, TB * 3])
        rms = sb("rms", [P, TB * 3])
        rinv = sb("rinv", [P, TB * 3])
        fn = sb("fn", [P, TB, P])
        ts_hl = sb("ts_split", [R, 2, L], F32R)
        bct = sb("bct", [SF, L])
        tp = [ps(f"tp{i}", [P, L]) for i in range(2)]
        ip = [ps(f"ip{i}", [P, L]) for i in range(NR)]
        fp = ps("fp", [P, TB * SF])
        ft_ps = ps("ft_ps", [P, L])

        fn_zero = sem("fn_zero")
        st_done, mv_done, ve_done = sem("st_done"), sem("mv_done"), sem("ve_done")
        std_done, rstd_done, xn_done = sem("std_done"), sem("rstd_done"), sem("xn_done")
        tp_done = sem("tp_done")
        hi_done, lo_done = sem("hi_done"), sem("lo_done")
        ip_done = sem("ip_done")
        xc_first = sem("xc_first")
        tap_step = sem("tap_step")
        taps_done = sem("taps_done")
        u_done, uhi_done, ulo_done = sem("u_done"), sem("uhi_done"), sem("ulo_done")
        g_done = sem("g_done")
        wx_used = sem("wx_used")
        u_out = [sem(f"u_out{i}") for i in range(2)]
        g_out = [sem(f"g_out{i}") for i in range(2)]
        feat_done, sq_done, rms_done, rinv_done, fn_done = (
            sem("feat_done"), sem("sq_done"), sem("rms_done"), sem("rinv_done"), sem("fn_done"))
        ftp_done = sem("ftp_done")
        tshi_done, tslo_done, bct_done = sem("tshi_done"), sem("tslo_done"), sem("bct_done")
        bc_out, ts_out = sem("bc_out"), sem("ts_out")
        KINDS = [(0, R), (R, R + NS), (R + NS, SF)]

        with nc.Block() as block:
            @block.sync
            def _(sp):
                with sp.Fori(0, NB) as b:
                    for m in range(DT):
                        sp.wait_ge(u_done, b * DT + (m + 1))
                        sp.dma_start(u_d[bass.ds(b, 1), m].rearrange("o p l -> (o p) l"),
                                     u[:, m % 2, :]).then_inc(u_out[m % 2], 16)
                        sp.wait_ge(g_done, b * DT + (m + 1))
                        sp.dma_start(g_d[bass.ds(b, 1), m].rearrange("o p l -> (o p) l"),
                                     g[:, m % 2, :]).then_inc(g_out[m % 2], 16)
                    sp.wait_ge(bct_done, b + 1)
                    sp.dma_start(bc_d[bass.ds(b, 1)].rearrange("o n l -> (o n) l"),
                                 bct[R:SF, :]).then_inc(bc_out, 16)
                    sp.wait_ge(tslo_done, b + 1)
                    sp.dma_start(ts_d[bass.ds(b, 1)].rearrange("o r s l -> (o r) s l"),
                                 ts_hl[:, :, :].bitcast(F32)).then_inc(ts_out, 16)
                sp.wait_ge(u_out[0], 16 * NB * DT // 2)
                sp.wait_ge(u_out[1], 16 * NB * DT // 2)
                sp.wait_ge(g_out[0], 16 * NB * DT // 2)
                sp.wait_ge(g_out[1], 16 * NB * DT // 2)
                sp.wait_ge(bc_out, 16 * NB)
                sp.wait_ge(ts_out, 16 * NB)

            @block.tensor
            def _(pe):
                with pe.Fori(0, NB) as b:
                    for k in range(KH):
                        for t in range(TB):
                            pe.wait_ge(xn_done, b * TB + (t + 1))
                            if t == 0 and k >= 2:
                                pe.wait_ge(lo_done, b * KH + (k - 1))
                            last = pe.transpose(tp[k % 2][:, P * t:P * (t + 1)],
                                                xn[:, t, P * k:P * (k + 1)], ident[:, :])
                        last.then_inc(tp_done, 1)

                    def features(m):
                        pe.wait_ge(ulo_done, b * DT + (m + 1))
                        pe.wait_ge(uhi_done, b * DT + (m + 1))
                        for t in range(TB):
                            s = slice(P * t, P * (t + 1))
                            last = products(pe, fp[:, SF * t:SF * (t + 1)], u_hi[:, m % 2, s],
                                            u_lo[:, m % 2, s], wx_hi[:, m, :], wx_lo[:, m, :],
                                            start=(m == 0 and t == 0), stop=(m == DT - 1),
                                            skip_group_check=True)
                        last.then_inc(wx_used, 1)

                    for j in range(2 * DT):
                        m, gate = j // 2, j % 2
                        e0 = gate * DI + m * P
                        if j >= NR:
                            jj = j - NR
                            pe.wait_ge(g_done if jj % 2 else taps_done, b * DT + (jj // 2 + 1))
                        for k in range(KH):
                            if j == 0:
                                pe.wait_ge(lo_done, b * KH + (k + 1))
                                pe.wait_ge(hi_done, b * KH + (k + 1))
                            last = products(pe, ip[j % NR][:, :], win_hi[:, k, e0:e0 + P],
                                            win_lo[:, k, e0:e0 + P], xt_hi[:, k, :], xt_lo[:, k, :],
                                            start=(k == 0), stop=(k == KH - 1))
                        last.then_inc(ip_done, 1)
                        if gate and m >= 1:
                            features(m - 1)
                    features(DT - 1)
                    for t in range(TB):
                        pe.wait_ge(fn_done, b * 3 * TB + 3 * (t + 1))
                        last = pe.transpose(ft_ps[:, P * t:P * (t + 1)], fn[:, t, :], ident[:, :])
                    last.then_inc(ftp_done, 1)

            @block.scalar
            def _(act):
                act.wait_ge(ve_done, 1)
                act.activation(std[:, :], var_e[:, :], ACT.Sqrt).then_inc(std_done, 1)
                with act.Fori(0, NB) as b:
                    for k in range(KH):
                        act.wait_ge(tp_done, b * KH + (k + 1))
                        act.activation(xt_hi[:, k, :], tp[k % 2][:, :], ACT.Copy).then_inc(hi_done, 1)
                    for m in range(DT):
                        act.wait_ge(ip_done, b * 2 * DT + (2 * m + 1))
                        if m >= 2:
                            act.wait_ge(u_done, b * DT + (m - 1))
                        act.activation(xc[:, m % 2, :], ip[(2 * m) % NR][:, :], ACT.Identity,
                                       bias=cb[:, m:m + 1], scale=cw[:, m, TAPS - 1:TAPS]).then_inc(xc_first, 1)
                        act.wait_ge(ip_done, b * 2 * DT + (2 * m + 2))
                        if m >= 2:
                            act.wait_ge(g_out[m % 2], b * (8 * DT) + 16 * (m // 2))
                        act.activation(g[:, m % 2, :], ip[(2 * m + 1) % NR][:, :], ACT.Silu).then_inc(g_done, 1)
                        act.wait_ge(taps_done, b * DT + (m + 1))
                        if m >= 2:
                            act.wait_ge(u_out[m % 2], b * (8 * DT) + 16 * (m // 2))
                            act.wait_ge(ulo_done, b * DT + (m - 1))
                            act.wait_ge(wx_used, b * DT + (m - 1))
                        act.activation(u[:, m % 2, :], xc[:, m % 2, :], ACT.Silu).then_inc(u_done, 1)
                        act.wait_ge(u_done, b * DT + (m + 1))
                        act.activation(u_hi[:, m % 2, :], u[:, m % 2, :], ACT.Copy).then_inc(uhi_done, 1)
                    act.wait_ge(wx_used, b * DT + DT)
                    act.activation(feat[:, :, :].rearrange("p t f -> p (t f)"), fp[:, :],
                                   ACT.Copy).then_inc(feat_done, 1)
                    act.wait_ge(sq_done, b * 3 * TB + 3 * TB)
                    act.activation(rms[:, :], ms[:, :], ACT.Sqrt).then_inc(rms_done, 1)
                    act.wait_ge(ftp_done, b + 1)
                    act.activation(ts_hl[:, 0, :], ft_ps[0:R, :], ACT.Copy).then_inc(tshi_done, 1)
                    act.activation(bct[R:SF, :], ft_ps[R:SF, :], ACT.Copy).then_inc(bct_done, 1)
                    act.wait_ge(u_out[0], b * (8 * DT) + 8 * DT)
                    act.wait_ge(u_out[1], b * (8 * DT) + 8 * DT)
                    act.wait_ge(g_out[0], b * (8 * DT) + 8 * DT)
                    act.wait_ge(g_out[1], b * (8 * DT) + 8 * DT)
                    act.wait_ge(bc_out, b * 16 + 16)
                    act.wait_ge(ts_out, b * 16 + 16)

            @block.vector
            def _(dve):
                dve.memset(fn[:, :, :], 0.0).then_inc(fn_zero, 1)
                dve.wait_ge(fn_zero, 1)
                layer_stats(dve, xall, stats, mv, var_e, st_done, mv_done, ve_done)
                dve.wait_ge(std_done, 1)
                dve.reciprocal(rstd[:, :], std[:, :]).then_inc(rstd_done, 1)
                dve.wait_ge(rstd_done, 1)
                with dve.Fori(0, NB) as b:
                    for t in range(TB):
                        dve.tensor_scalar(xn[:, t, :], xall[:, bass.ds(b * TB + t, 1), :].rearrange(
                            "p o h -> p (o h)"), mv[:, bass.ds(b * TB + t, 1), 0],
                            rstd[:, bass.ds(b * TB + t, 1)],
                            ALU.subtract, ALU.mult).then_inc(xn_done, 1)
                    for k in range(KH):
                        dve.wait_ge(hi_done, b * KH + (k + 1))
                        dve.tensor_tensor(xt_lo[:, k, :], tp[k % 2][:, :], xt_hi[:, k, :].bitcast(F32),
                                          ALU.subtract).then_inc(lo_done, 1)
                    for m in range(DT):
                        for j in range(TAPS - 1):
                            s = TAPS - 1 - j
                            if j == 0:
                                dve.wait_ge(xc_first, b * DT + (m + 1))
                            else:
                                dve.wait_ge(tap_step, b * DT * (TAPS - 2) + m * (TAPS - 2) + j)
                            done = dve.scalar_tensor_tensor(
                                out=xc[:, m % 2, s:], in0=ip[(2 * m) % NR][:, 0:L - s],
                                scalar=cw[:, m, j:j + 1], in1=xc[:, m % 2, s:], op0=ALU.mult, op1=ALU.add)
                            done.then_inc(taps_done if j == TAPS - 2 else tap_step, 1)
                    dve.wait_ge(feat_done, b + 1)
                    for t in range(TB):
                        for i, (f0, f1) in enumerate(KINDS):
                            if t + i:
                                dve.wait_ge(sq_done, b * 3 * TB + (3 * t + i))
                            dve.tensor_tensor_reduce(fsq[:, f0:f1], feat[:, t, f0:f1], feat[:, t, f0:f1],
                                                     1.0 / (f1 - f0), RMS_EPS, ALU.mult, ALU.add,
                                                     ms[:, 3 * t + i:3 * t + i + 1]).then_inc(sq_done, 1)
                    dve.wait_ge(rms_done, b + 1)
                    dve.reciprocal(rinv[:, :], rms[:, :]).then_inc(rinv_done, 1)
                    dve.wait_ge(rinv_done, b + 1)
                    for t in range(TB):
                        for i, (f0, f1) in enumerate(KINDS):
                            dve.tensor_scalar(fn[:, t, f0:f1], feat[:, t, f0:f1],
                                              rinv[:, 3 * t + i:3 * t + i + 1], None,
                                              ALU.mult).then_inc(fn_done, 1)
                    dve.wait_ge(tshi_done, b + 1)
                    dve.tensor_tensor(ts_hl[:, 1, :], ft_ps[0:R, :], ts_hl[:, 0, :].bitcast(F32),
                                      ALU.subtract).then_inc(tslo_done, 1)

            @block.gpsimd
            def _(pool):
                with pool.Fori(0, NB) as b:
                    for m in range(DT):
                        pool.wait_ge(uhi_done, b * DT + (m + 1))
                        if m >= 2:
                            pool.wait_ge(wx_used, b * DT + (m - 1))
                        pool.tensor_tensor(u_lo[:, m % 2, :], u[:, m % 2, :],
                                           u_hi[:, m % 2, :].bitcast(F32), ALU.subtract).then_inc(ulo_done, 1)


def scan(nc, tensors, xall, ident, a_neg, dsk, wdt_hi, wdt_lo, ts_hl, w_out, u_d, g_d, bc_d, ts_d):
    RA, RB, RP, NQ = 4, 4, 4, 4
    UNITS = DT * NS
    with ExitStack() as c:
        sb, ps, sem = tensors(c)
        wo_hi, wo_lo = sb("wo_hi", [P, DT, H], F32R), sb("wo_lo", [P, DT, H], F32R)
        bb, cc = sb("bb", [P, NS, L]), sb("cc", [P, NS, L])
        u, g = sb("u_s", [P, 2, L]), sb("g_s", [P, 2, L])
        dt, dtu = sb("dt", [P, 2, L]), sb("dtu", [P, 2, L])
        sp1, sp2 = sb("sp1", [P, L]), sb("sp2", [P, L])
        decay = sb("decay", [P, RA, L])
        drive = sb("drive", [P, RB, L])
        hst = sb("hst", [P, 2, L])
        prod = sb("prod", [P, RP, L])
        yg = sb("yg", [P, L])
        yg_hi, yg_lo = sb("yg_hi", [P, 2, L], F32R), sb("yg_lo", [P, 2, L], F32R)
        dtp = ps("dtp", [P, L])
        yp = [ps(f"yp{i}", [P, L]) for i in range(2)]
        op = [ps(f"op{t}", [P, H]) for t in range(TB)]

        wo_in = [sem(f"wo_in{i}") for i in range(2)]
        wo_split, wo_rest = sem("wo_split"), sem("wo_rest")
        bb_in = [sem(f"bb_in{q}") for q in range(NQ)]
        cc_in = [sem(f"cc_in{q}") for q in range(NQ)]
        u_in = [sem(f"u_in{i}") for i in range(2)]
        g_in = [sem(f"g_in{i}") for i in range(2)]
        ts_in = sem("ts_in")
        dtp_done = sem("dtp_done")
        abs_done, e_done, w_done, ln_done = sem("abs_done"), sem("e_done"), sem("w_done"), sem("ln_done")
        round_done, log_done, dt_done, dtu_done = sem("round_done"), sem("log_done"), sem("dt_done"), sem("dtu_done")
        decay_done, drive_done, h_done, prod_done = sem("decay_done"), sem("drive_done"), sem("h_done"), sem("prod_done")
        unit_summed = sem("unit_summed")
        skip_done, yg_done, yhi_done, ylo_done = sem("skip_done"), sem("yg_done"), sem("yhi_done"), sem("ylo_done")
        op_done, res_done = sem("op_done"), sem("res_done")
        batch_over = sem("batch_over")

        with nc.Block() as block:
            @block.sync
            def _(sp):
                half = DT // 2
                for i, dst in enumerate((bb, cc)):
                    sp.dma_start(dst[:, 0:half, :], w_out[:, half * i:half * (i + 1), :]).then_inc(wo_in[i], 16)
                sp.wait_ge(wo_rest, 2)
                with sp.Fori(0, NB) as b:
                    sp.dma_start(ts_hl[0:R, :, :].bitcast(F32),
                                 ts_d[bass.ds(b, 1)].rearrange("o r s l -> (o r) s l")).then_inc(ts_in, 16)
                    for q in range(NQ):
                        s = slice(q * NS // NQ, (q + 1) * NS // NQ)
                        for dst, off, done in ((bb, 0, bb_in), (cc, NS, cc_in)):
                            src = bc_d[bass.ds(b, 1), off + s.start:off + s.stop].rearrange(
                                "o n l -> o (n l)").broadcast_to([P, NS // NQ * L])
                            sp.dma_start(dst[:, s, :].rearrange("p n l -> p (n l)"), src).then_inc(done[q], 16)
                    for d in range(DT):
                        if d >= 2:
                            sp.wait_ge(yg_done, b * DT + (d - 1))
                            sp.wait_ge(skip_done, b * DT + (d - 1))
                            sp.wait_ge(dtu_done, b * DT + (d - 1))
                        sp.dma_start(u[:, d % 2, :], u_d[bass.ds(b, 1), d].rearrange(
                            "o p l -> (o p) l")).then_inc(u_in[d % 2], 16)
                        sp.dma_start(g[:, d % 2, :], g_d[bass.ds(b, 1), d].rearrange(
                            "o p l -> (o p) l")).then_inc(g_in[d % 2], 16)
                    sp.wait_ge(res_done, b * TB + TB)
                    sp.sem_inc(batch_over, 1)

            @block.tensor
            def _(pe):
                with pe.Fori(0, NB) as b:
                    def dt_product(d):
                        if d == 0:
                            pe.wait_ge(ts_in, b * 16 + 16)
                        if d >= 1:
                            pe.wait_ge(dt_done, b * DT + d)
                            pe.wait_ge(abs_done, b * DT + d)
                        s = slice(P * d, P * (d + 1))
                        products(pe, dtp[:, :], wdt_hi[:, s], wdt_lo[:, s], ts_hl[:, 0, :],
                                 ts_hl[:, 1, :], start=True, stop=True).then_inc(dtp_done, 1)

                    def out_product(d):
                        pe.wait_ge(yhi_done, b * DT + (d + 1))
                        pe.wait_ge(ylo_done, b * DT + (d + 1))
                        for t in range(TB):
                            s = slice(P * t, P * (t + 1))
                            last = products(pe, op[t][:, :], yg_hi[:, d % 2, s], yg_lo[:, d % 2, s],
                                            wo_hi[:, d, :], wo_lo[:, d, :], start=(d == 0), stop=(d == DT - 1))
                        last.then_inc(op_done, 1)

                    dt_product(0)
                    for d in range(DT):
                        for n in range(NS):
                            k = d * NS + n
                            pe.wait_ge(prod_done, b * UNITS + (k + 1))
                            if n == 0 and d >= 2:
                                pe.wait_ge(skip_done, b * DT + (d - 1))
                            pe.matmul(yp[d % 2][:, :], ident[:, :], prod[:, k % RP, :], start=(n == 0),
                                      stop=(n == NS - 1)).then_inc(unit_summed, 1)
                            if n == 0 and d + 1 < DT:
                                dt_product(d + 1)
                            if n == 8 and d >= 1:
                                out_product(d - 1)
                    out_product(DT - 1)

            @block.scalar
            def _(act):
                half = DT // 2
                for i, src in enumerate((bb, cc)):
                    act.wait_ge(wo_in[i], 16)
                    act.activation(wo_hi[:, half * i:half * (i + 1), :], src[:, 0:half, :],
                                   ACT.Copy).then_inc(wo_split, 1)
                with act.Fori(0, NB) as b:
                    def softplus_exp(d):
                        act.wait_ge(dtp_done, b * DT + (d + 1))
                        if d >= 1:
                            act.wait_ge(round_done, b * DT + d)
                            act.wait_ge(log_done, b * DT + d)
                            act.wait_ge(dt_done, b * DT + d)
                        act.activation(sp1[:, :], dtp[:, :], ACT.Abs).then_inc(abs_done, 1)
                        act.wait_ge(abs_done, b * DT + (d + 1))
                        act.activation(sp1[:, :], sp1[:, :], ACT.Exp, scale=-1.0).then_inc(e_done, 1)

                    def softplus_log(d):
                        act.wait_ge(round_done, b * DT + (d + 1))
                        act.activation(sp2[:, :], sp2[:, :], ACT.Ln).then_inc(ln_done, 1)

                    def split_y(d):
                        act.wait_ge(yg_done, b * DT + (d + 1))
                        if d >= 2:
                            act.wait_ge(op_done, b * DT + (d - 1))
                        act.activation(yg_hi[:, d % 2, :], yg[:, :], ACT.Copy).then_inc(yhi_done, 1)

                    softplus_exp(0)
                    softplus_log(0)
                    for d in range(DT):
                        for n in range(NS):
                            k = d * NS + n
                            if n == 0:
                                act.wait_ge(dt_done, b * DT + (d + 1))
                            if k >= RA:
                                act.wait_ge(h_done, b * UNITS + (k - RA + 1))
                            act.activation(decay[:, k % RA, :], dt[:, d % 2, :], ACT.Exp,
                                           scale=a_neg[:, d, n:n + 1]).then_inc(decay_done, 1)
                            if n == 7 and d >= 1:
                                split_y(d - 1)
                            if n == 5 and d + 1 < DT:
                                softplus_exp(d + 1)
                            if n == 9 and d + 1 < DT:
                                softplus_log(d + 1)
                    split_y(DT - 1)

            @block.vector
            def _(dve):
                half = DT // 2
                for i, src in enumerate((bb, cc)):
                    dve.wait_ge(wo_split, i + 1)
                    dve.tensor_tensor(wo_lo[:, half * i:half * (i + 1), :], src[:, 0:half, :],
                                      wo_hi[:, half * i:half * (i + 1), :].bitcast(F32),
                                      ALU.subtract).then_inc(wo_rest, 1)
                with dve.Fori(0, NB) as b:
                    def softplus_w(d):
                        dve.wait_ge(e_done, b * DT + (d + 1))
                        dve.tensor_scalar(sp2[:, :], sp1[:, :], 1.0, None, ALU.add).then_inc(w_done, 1)
                        dve.wait_ge(w_done, b * DT + (d + 1))
                        dve.scalar_tensor_tensor(out=sp1[:, :], in0=sp2[:, :], scalar=-1.0, in1=sp1[:, :],
                                                 op0=ALU.add, op1=ALU.subtract).then_inc(round_done, 1)

                    def softplus_sum(d):
                        dve.wait_ge(ln_done, b * DT + (d + 1))
                        dve.tensor_tensor(sp2[:, :], sp2[:, :], sp1[:, :], ALU.subtract).then_inc(log_done, 1)
                        dve.wait_ge(log_done, b * DT + (d + 1))
                        if d >= 2:
                            dve.wait_ge(decay_done, b * UNITS + NS * (d - 1))
                            dve.wait_ge(dtu_done, b * DT + (d - 1))
                        dve.scalar_tensor_tensor(out=dt[:, d % 2, :], in0=dtp[:, :], scalar=0.0,
                                                 in1=sp2[:, :], op0=ALU.max, op1=ALU.add).then_inc(dt_done, 1)

                    def gate_y(d):
                        dve.wait_ge(unit_summed, b * UNITS + NS * (d + 1))
                        dve.wait_ge(u_in[d % 2], b * (8 * DT) + 16 * (d // 2 + 1))
                        if d >= 1:
                            dve.wait_ge(yhi_done, b * DT + d)
                            dve.wait_ge(ylo_done, b * DT + d)
                        dve.scalar_tensor_tensor(out=yg[:, :], in0=u[:, d % 2, :], scalar=dsk[:, d:d + 1],
                                                 in1=yp[d % 2][:, :], op0=ALU.mult,
                                                 op1=ALU.add).then_inc(skip_done, 1)
                        dve.wait_ge(skip_done, b * DT + (d + 1))
                        dve.wait_ge(g_in[d % 2], b * (8 * DT) + 16 * (d // 2 + 1))
                        dve.tensor_tensor(yg[:, :], yg[:, :], g[:, d % 2, :], ALU.mult).then_inc(yg_done, 1)

                    def scan_unit(k):
                        dve.wait_ge(decay_done, b * UNITS + (k + 1))
                        dve.wait_ge(drive_done, b * UNITS + (k + 1))
                        if k >= 2:
                            dve.wait_ge(prod_done, b * UNITS + (k - 1))
                        dve.tensor_tensor_scan(hst[:, k % 2, :], decay[:, k % RA, :], drive[:, k % RB, :],
                                               0.0, ALU.mult, ALU.add).then_inc(h_done, 1)

                    def read_unit(k):
                        if k < NS and k % (NS // NQ) == 0:
                            dve.wait_ge(cc_in[k // (NS // NQ)], b * 16 + 16)
                        dve.wait_ge(h_done, b * UNITS + (k + 1))
                        if k >= RP:
                            dve.wait_ge(unit_summed, b * UNITS + (k - RP + 1))
                        dve.tensor_tensor(prod[:, k % RP, :], hst[:, k % 2, :], cc[:, k % NS, :],
                                          ALU.mult).then_inc(prod_done, 1)

                    softplus_w(0)
                    softplus_sum(0)
                    for k in range(UNITS):
                        d, n = divmod(k, NS)
                        scan_unit(k)
                        if k >= 1:
                            read_unit(k - 1)
                        if n == 3 and d >= 1:
                            gate_y(d - 1)
                        if n == 5 and d + 1 < DT:
                            softplus_w(d + 1)
                        if n == 10 and d + 1 < DT:
                            softplus_sum(d + 1)
                    read_unit(UNITS - 1)
                    gate_y(DT - 1)
                    for t in range(TB):
                        dve.wait_ge(op_done, b * DT + DT)
                        xs = xall[:, bass.ds(b * TB + t, 1), :].rearrange("p o h -> p (o h)")
                        dve.tensor_tensor(xs, op[t][:, :], xs, ALU.add).then_inc(res_done, 1)

            @block.gpsimd
            def _(pool):
                with pool.Fori(0, NB) as b:
                    def input_gain(d):
                        pool.wait_ge(dt_done, b * DT + (d + 1))
                        pool.wait_ge(u_in[d % 2], b * (8 * DT) + 16 * (d // 2 + 1))
                        if d >= 2:
                            pool.wait_ge(drive_done, b * UNITS + NS * (d - 1))
                        pool.tensor_tensor(dtu[:, d % 2, :], dt[:, d % 2, :], u[:, d % 2, :],
                                           ALU.mult).then_inc(dtu_done, 1)

                    def rest_y(d):
                        pool.wait_ge(yhi_done, b * DT + (d + 1))
                        if d >= 2:
                            pool.wait_ge(op_done, b * DT + (d - 1))
                        pool.tensor_tensor(yg_lo[:, d % 2, :], yg[:, :], yg_hi[:, d % 2, :].bitcast(F32),
                                           ALU.subtract).then_inc(ylo_done, 1)

                    input_gain(0)
                    for k in range(UNITS):
                        d, n = divmod(k, NS)
                        if n == 0:
                            pool.wait_ge(dtu_done, b * DT + (d + 1))
                        if k < NS and k % (NS // NQ) == 0:
                            pool.wait_ge(bb_in[k // (NS // NQ)], b * 16 + 16)
                        if k >= RB:
                            pool.wait_ge(h_done, b * UNITS + (k - RB + 1))
                        pool.tensor_tensor(drive[:, k % RB, :], dtu[:, d % 2, :], bb[:, n, :],
                                           ALU.mult).then_inc(drive_done, 1)
                        if n == 9 and d >= 1:
                            rest_y(d - 1)
                        if n == 12 and d + 1 < DT:
                            input_gain(d + 1)
                    rest_y(DT - 1)


def ffn(nc, tensors, xall, ident, qw_gu, qz_gu, sc_gu, gi_gu, qw_d, qz_d, sc_d, gi_d, out):
    with ExitStack() as c:
        sb, ps, sem = tensors(c)
        wg_hi, wg_lo = sb("wg_hi", [P, KH, 2 * INTER], F32R), sb("wg_lo", [P, KH, 2 * INTER], F32R)
        wd_hi, wd_lo = sb("wd_hi", [P, FT, H], F32R), sb("wd_lo", [P, FT, H], F32R)
        dequant(nc, tensors, H, NG, 2 * INTER, "gu", qw_gu, qz_gu, sc_gu, gi_gu, wg_hi, wg_lo)
        dequant(nc, tensors, INTER, NGD, H, "down", qw_d, qz_d, sc_d, gi_d, wd_hi, wd_lo)
        swiglu(nc, tensors, xall, ident, wg_hi, wg_lo, wd_hi, wd_lo, out)


def dequant(nc, tensors, K, G, N, tag, qw, qz, sc, gi, w_hi, w_lo):
    CH = 512
    units = [(k0, n0) for k0 in range(0, K, P) for n0 in range(0, N, CH)]
    with ExitStack() as c:
        sb, ps, sem = tensors(c)
        hot_i = sb(f"{tag}_hot_i", [G, K], I32)
        hot = sb(f"{tag}_hot", [G, K])
        neg = sb(f"{tag}_neg", [G, K])
        hot_r = sb(f"{tag}_hot_r", [G, K], F32R)
        pid = sb(f"{tag}_pid", [P, 1], U32)
        pidf = sb(f"{tag}_pidf", [P, 1])
        sh = sb(f"{tag}_sh", [P, 1], U32)
        CS = min(N, 1376)
        zi = sb(f"{tag}_zi", [G, CS // QC], U32)
        zn = sb(f"{tag}_zn", [G, CS // QC], U32)
        zr = sb(f"{tag}_zr", [G, CS], F32R)
        sf = sb(f"{tag}_sf", [G, CS])
        s_hi, s_lo = sb(f"{tag}_s_hi", [G, CS], F32R), sb(f"{tag}_s_lo", [G, CS], F32R)
        qr = sb(f"{tag}_qr", [P, 2, CH], U32)
        wf = sb(f"{tag}_wf", [P, 2, CH])
        zp = [ps(f"{tag}_zp{i}", [P, CH]) for i in range(2)]
        scp = [ps(f"{tag}_scp{i}", [P, CH]) for i in range(2)]
        pid_done, sh_done = sem(f"{tag}_pid_done"), sem(f"{tag}_sh_done")
        gi_in, z_in, s_in = sem(f"{tag}_gi_in"), sem(f"{tag}_z_in"), sem(f"{tag}_s_in")
        q_in = [sem(f"{tag}_q_in{i}") for i in range(2)]
        hot_step, z_step, s_step = sem(f"{tag}_hot_step"), sem(f"{tag}_z_step"), sem(f"{tag}_s_step")
        picked = sem(f"{tag}_picked")
        nib_done, sub_done, w_done = sem(f"{tag}_nib_done"), sem(f"{tag}_sub_done"), sem(f"{tag}_w_done")
        hi_done, lo_done = sem(f"{tag}_hi_done"), sem(f"{tag}_lo_done")
        halves = N // CS
        units = [(h, k0, n0) for h in range(halves) for k0 in range(0, K, P) for n0 in range(0, CS, CH)]
        per_half = len(units) // halves
        size = lambda k0, n0: (min(P, K - k0), min(CH, CS - n0))
        ZOPS = 2 * QC

        with nc.Block() as block:
            @block.sync
            def _(sp):
                sp.dma_start(hot_i[:, :], gi.broadcast_to([G, K])).then_inc(gi_in, 16)
                for i, (h, k0, n0) in enumerate(units):
                    if i % per_half == 0:
                        if h:
                            sp.wait_ge(z_step, ZOPS * h)
                            sp.wait_ge(s_step, 2 * h)
                        sp.dma_start(zi[:, :], qz[:, h * CS // QC:(h + 1) * CS // QC]).then_inc(z_in, 16)
                        sp.dma_start(sf[:, :], sc[:, h * CS:(h + 1) * CS]).then_inc(s_in, 16)
                    kk, nn = size(k0, n0)
                    if i >= 2:
                        sp.wait_ge(sub_done, i - 1)
                    src = qw[k0 // QC:(k0 + kk) // QC, h * CS + n0:h * CS + n0 + nn]
                    sp.dma_start(qr[0:kk, i % 2, 0:nn],
                                 src.unsqueeze(1).broadcast_to([kk // QC, QC, nn])).then_inc(q_in[i % 2], 16)

            @block.gpsimd
            def _(pool):
                pool.iota(pid[:, :], pattern=[[0, 1]], base=0, channel_multiplier=1).then_inc(pid_done, 1)
                for i, (h, k0, n0) in enumerate(units):
                    kk, nn = size(k0, n0)
                    if i % 2:
                        pool.wait_ge(hi_done, i + 1)
                        c0 = h * CS + n0
                        pool.tensor_tensor(w_lo[0:kk, k0 // P, c0:c0 + nn], wf[0:kk, i % 2, 0:nn],
                                           w_hi[0:kk, k0 // P, c0:c0 + nn].bitcast(F32),
                                           ALU.subtract).then_inc(lo_done, 1)

            @block.tensor
            def _(pe):
                for i, (h, k0, n0) in enumerate(units):
                    kk, nn = size(k0, n0)
                    if i == 0:
                        pe.wait_ge(hot_step, 6)
                    if i % per_half == 0:
                        pe.wait_ge(z_step, ZOPS * (h + 1))
                        pe.wait_ge(s_step, 2 * (h + 1))
                    if i >= 2:
                        pe.wait_ge(w_done, i - 1)
                    pick = hot_r[:, k0:k0 + kk]
                    pe.matmul(zp[i % 2][0:kk, 0:nn], pick, zr[:, n0:n0 + nn], start=True, stop=True)
                    pe.matmul(scp[i % 2][0:kk, 0:nn], pick, s_hi[:, n0:n0 + nn], start=True, stop=False)
                    pe.matmul(scp[i % 2][0:kk, 0:nn], pick, s_lo[:, n0:n0 + nn], start=False,
                              stop=True).then_inc(picked, 1)

            @block.scalar
            def _(act):
                for i, (h, k0, n0) in enumerate(units):
                    kk, nn = size(k0, n0)
                    c0 = h * CS + n0
                    act.wait_ge(w_done, i + 1)
                    act.activation(w_hi[0:kk, k0 // P, c0:c0 + nn], wf[0:kk, i % 2, 0:nn],
                                   ACT.Copy).then_inc(hi_done, 1)

            @block.vector
            def _(dve):
                dve.wait_ge(pid_done, 1)
                dve.tensor_scalar(sh[:, :], pid[:, :], QC - 1, 2, ALU.bitwise_and,
                                  ALU.logical_shift_left).then_inc(sh_done, 1)
                dve.tensor_copy(pidf[:, :], pid[:, :]).then_inc(sh_done, 1)
                dve.wait_ge(gi_in, 16)
                dve.tensor_copy(hot[:, :], hot_i[:, :]).then_inc(hot_step, 1)
                dve.wait_ge(hot_step, 1)
                dve.tensor_scalar(neg[:, :], hot[:, :], 0.0, float(G), ALU.is_lt, ALU.mult).then_inc(hot_step, 1)
                dve.wait_ge(hot_step, 2)
                dve.tensor_tensor(hot[:, :], hot[:, :], neg[:, :], ALU.add).then_inc(hot_step, 1)
                dve.wait_ge(hot_step, 3)
                dve.tensor_scalar(hot[:, :], hot[:, :], 0.0, float(G - 1), ALU.max, ALU.min).then_inc(hot_step, 1)
                dve.wait_ge(hot_step, 4)
                dve.wait_ge(sh_done, 2)
                dve.tensor_scalar(hot[:, :], hot[:, :], pidf[0:G, 0:1], None, ALU.is_equal).then_inc(hot_step, 1)
                dve.wait_ge(hot_step, 5)
                dve.tensor_copy(hot_r[:, :], hot[:, :]).then_inc(hot_step, 1)
                for i, (h, k0, n0) in enumerate(units):
                    kk, nn = size(k0, n0)
                    if i % per_half == 0:
                        if h:
                            dve.wait_ge(picked, i)
                        dve.wait_ge(z_in, 16 * (h + 1))
                        for j in range(QC):
                            if h or j:
                                dve.wait_ge(z_step, ZOPS * h + 2 * j)
                            dve.tensor_scalar(zn[:, :], zi[:, :], 4 * j, 15, ALU.logical_shift_right,
                                              ALU.bitwise_and).then_inc(z_step, 1)
                            dve.wait_ge(z_step, ZOPS * h + 2 * j + 1)
                            dve.tensor_scalar(zr[:, :].rearrange("g (c j) -> g c j", j=QC)[:, :, j], zn[:, :],
                                              1.0, None, ALU.add).then_inc(z_step, 1)
                        dve.wait_ge(s_in, 16 * (h + 1))
                        dve.tensor_copy(s_hi[:, :], sf[:, :]).then_inc(s_step, 1)
                        dve.wait_ge(s_step, 2 * h + 1)
                        dve.tensor_tensor(s_lo[:, :], sf[:, :], s_hi[:, :].bitcast(F32),
                                          ALU.subtract).then_inc(s_step, 1)
                    dve.wait_ge(q_in[i % 2], 16 * (i // 2 + 1))
                    q = qr[0:kk, i % 2, 0:nn]
                    dve.tensor_scalar(q, q, sh[0:kk, 0:1], 15, ALU.logical_shift_right,
                                      ALU.bitwise_and).then_inc(nib_done, 1)
                    dve.wait_ge(nib_done, i + 1)
                    dve.wait_ge(picked, i + 1)
                    if i >= 2:
                        if i % 2:
                            dve.wait_ge(lo_done, i // 2)
                        dve.wait_ge(hi_done, i - 1)
                    w = wf[0:kk, i % 2, 0:nn]
                    dve.tensor_tensor(w, q, zp[i % 2][0:kk, 0:nn], ALU.subtract).then_inc(sub_done, 1)
                    dve.wait_ge(sub_done, i + 1)
                    dve.tensor_tensor(w, w, scp[i % 2][0:kk, 0:nn], ALU.mult).then_inc(w_done, 1)
                    if i % 2 == 0:
                        c0 = h * CS + n0
                        dve.wait_ge(hi_done, i + 1)
                        dve.tensor_tensor(w_lo[0:kk, k0 // P, c0:c0 + nn], w,
                                          w_hi[0:kk, k0 // P, c0:c0 + nn].bitcast(F32), ALU.subtract)


def swiglu(nc, tensors, xall, ident, wg_hi, wg_lo, wd_hi, wd_lo, out):
    with ExitStack() as c:
        sb, ps, sem = tensors(c)
        stats = sb("stats2", [P, NB * TB, 6])
        mv = sb("mv2", [P, NB * TB, 2])
        var_e, std, rstd = sb("var_e2", [P, NB * TB]), sb("std2", [P, NB * TB]), sb("rstd2", [P, NB * TB])
        xn = sb("xn2", [P, TB, H])
        xt_hi, xt_lo = sb("xt_hi2", [P, KH, L], F32R), sb("xt_lo2", [P, KH, L], F32R)
        sg = sb("sg", [P, L])
        hf = sb("hf", [P, L])
        h_hi, h_lo = sb("h_hi", [P, 2, L], F32R), sb("h_lo", [P, 2, L], F32R)
        gp = [ps(f"gp{i}", [P, L]) for i in range(2)]
        up = [ps(f"up{i}", [P, L]) for i in range(2)]
        tp = [gp[0], up[0], gp[1], up[1]]
        dp = [ps(f"dp{t}", [P, H]) for t in range(TB)]
        st_done, mv_done, ve_done = sem("st2_done"), sem("mv2_done"), sem("ve2_done")
        std_done, rstd_done, xn_done = sem("std2_done"), sem("rstd2_done"), sem("xn2_done")
        tp_done, hi_done, lo_done = sem("tp2_done"), sem("hi2_done"), sem("lo2_done")
        gu_done = sem("gu_done")
        sg_done, hf_done, hhi_done, hlo_done = sem("sg_done"), sem("hf_done"), sem("hhi_done"), sem("hlo_done")
        dp_done, res_done, out_done = sem("dp_done"), sem("res2_done"), sem("out_done")

        with nc.Block() as block:
            @block.sync
            def _(sp):
                with sp.Fori(0, NB) as b:
                    sp.wait_ge(res_done, b * TB + TB)
                    sp.dma_start(out[bass.ds(b, 1)].rearrange("o p t h -> (o p) t h"),
                                 xall[:, bass.ds(b * TB, TB), :]).then_inc(out_done, 16)
                sp.wait_ge(out_done, 16 * NB)

            @block.tensor
            def _(pe):
                with pe.Fori(0, NB) as b:
                    for k in range(KH):
                        for t in range(TB):
                            if k == 0:
                                pe.wait_ge(xn_done, b * TB + (t + 1))
                            last = pe.transpose(tp[k][:, P * t:P * (t + 1)], xn[:, t, P * k:P * (k + 1)],
                                                ident[:, :])
                        last.then_inc(tp_done, 1)

                    def down(f):
                        pe.wait_ge(hhi_done, b * FT + (f + 1))
                        pe.wait_ge(hlo_done, b * FT + (f + 1))
                        r = rows(f)
                        for t in range(TB):
                            s = slice(P * t, P * (t + 1))
                            last = products(pe, dp[t][:, :], h_hi[0:r, f % 2, s], h_lo[0:r, f % 2, s],
                                            wd_hi[0:r, f, :], wd_lo[0:r, f, :],
                                            start=(f == 0), stop=(f == FT - 1))
                        last.then_inc(dp_done, 1)

                    for f in range(FT):
                        r = rows(f)
                        if f == 0:
                            pe.wait_ge(hi_done, b * KH + KH)
                            pe.wait_ge(lo_done, b * KH + KH)
                        if f >= 2:
                            pe.wait_ge(sg_done, b * FT + (f - 1))
                            pe.wait_ge(hf_done, b * FT + (f - 1))
                        for bank, c0 in ((gp, 0), (up, INTER)):
                            s = slice(c0 + P * f, c0 + P * f + r)
                            for k in range(KH):
                                last = products(pe, bank[f % 2][0:r, :], wg_hi[:, k, s], wg_lo[:, k, s],
                                                xt_hi[:, k, :], xt_lo[:, k, :], start=(k == 0),
                                                stop=(k == KH - 1))
                        last.then_inc(gu_done, 1)
                        if f >= 1:
                            down(f - 1)
                    down(FT - 1)

            @block.scalar
            def _(act):
                act.wait_ge(ve_done, 1)
                act.activation(std[:, :], var_e[:, :], ACT.Sqrt).then_inc(std_done, 1)
                with act.Fori(0, NB) as b:
                    for k in range(KH):
                        act.wait_ge(tp_done, b * KH + (k + 1))
                        act.activation(xt_hi[:, k, :], tp[k][:, :], ACT.Copy).then_inc(hi_done, 1)
                    for f in range(FT):
                        r = rows(f)
                        act.wait_ge(gu_done, b * FT + (f + 1))
                        if f >= 1:
                            act.wait_ge(hf_done, b * FT + f)
                        act.activation(sg[0:r, :], gp[f % 2][0:r, :], ACT.Silu).then_inc(sg_done, 1)
                        act.wait_ge(hf_done, b * FT + (f + 1))
                        if f >= 2:
                            act.wait_ge(dp_done, b * FT + (f - 1))
                        act.activation(h_hi[0:r, f % 2, :], hf[0:r, :], ACT.Copy).then_inc(hhi_done, 1)

            @block.gpsimd
            def _(pool):
                with pool.Fori(0, NB) as b:
                    for f in range(FT):
                        r = rows(f)
                        pool.wait_ge(hhi_done, b * FT + (f + 1))
                        if f >= 2:
                            pool.wait_ge(dp_done, b * FT + (f - 1))
                        pool.tensor_tensor(h_lo[0:r, f % 2, :], hf[0:r, :], h_hi[0:r, f % 2, :].bitcast(F32),
                                           ALU.subtract).then_inc(hlo_done, 1)

            @block.vector
            def _(dve):
                layer_stats(dve, xall, stats, mv, var_e, st_done, mv_done, ve_done)
                dve.wait_ge(std_done, 1)
                dve.reciprocal(rstd[:, :], std[:, :]).then_inc(rstd_done, 1)
                dve.wait_ge(rstd_done, 1)
                with dve.Fori(0, NB) as b:
                    for t in range(TB):
                        dve.tensor_scalar(xn[:, t, :], xall[:, bass.ds(b * TB + t, 1), :].rearrange(
                            "p o h -> p (o h)"), mv[:, bass.ds(b * TB + t, 1), 0],
                            rstd[:, bass.ds(b * TB + t, 1)],
                            ALU.subtract, ALU.mult).then_inc(xn_done, 1)
                    for k in range(KH):
                        dve.wait_ge(hi_done, b * KH + (k + 1))
                        dve.tensor_tensor(xt_lo[:, k, :], tp[k][:, :], xt_hi[:, k, :].bitcast(F32),
                                          ALU.subtract).then_inc(lo_done, 1)
                    for f in range(FT):
                        r = rows(f)
                        dve.wait_ge(sg_done, b * FT + (f + 1))
                        if f >= 1:
                            dve.wait_ge(hhi_done, b * FT + f)
                            dve.wait_ge(hlo_done, b * FT + f)
                        dve.tensor_tensor(hf[0:r, :], sg[0:r, :], up[f % 2][0:r, :],
                                          ALU.mult).then_inc(hf_done, 1)
                    dve.wait_ge(dp_done, b * FT + FT)
                    for t in range(TB):
                        xs = xall[:, bass.ds(b * TB + t, 1), :].rearrange("p o h -> p (o h)")
                        dve.tensor_tensor(xs, dp[t][:, :], xs, ALU.add).then_inc(res_done, 1)


def kernel(**inputs):
    import numpy as np
    import concourse.bacc as bacc
    from concourse.bass_utils import run_bass_kernel_spmd as run

    get = lambda n: np.asarray(inputs[n])
    lay = {
        "x": get("L0_attn_hidden_states").reshape(NB, TB, P, H).transpose(0, 2, 1, 3),
        "w_in": get("L0_attn_W_in").T.reshape(KH, P, 2 * DI).transpose(1, 0, 2),
        "conv_w": get("L0_attn_conv_w").reshape(DT, P, TAPS).transpose(1, 0, 2),
        "conv_b": get("L0_attn_conv_b").reshape(DT, P).T,
        "w_x": get("L0_attn_W_x").T.reshape(DT, P, SF).transpose(1, 0, 2),
        "w_dt": np.concatenate([get("L0_attn_W_dt").T, get("L0_attn_b_dt")[None]], 0),
        "a_log": get("L0_attn_A_log").reshape(DT, P, NS).transpose(1, 0, 2),
        "d_skip": get("L0_attn_D").reshape(DT, P).T,
        "w_out": get("L0_attn_W_out").T.reshape(DT, P, H).transpose(1, 0, 2),
        "qw_gu": get("L0_ffn_qweight_gu"), "qz_gu": get("L0_ffn_qzeros_gu"),
        "sc_gu": get("L0_ffn_scales_gu"), "gi_gu": get("L0_ffn_g_idx_gu")[None],
        "qw_d": get("L0_ffn_qweight_down"), "qz_d": get("L0_ffn_qzeros_down"),
        "sc_d": get("L0_ffn_scales_down"), "gi_d": get("L0_ffn_g_idx_down")[None],
    }
    nc = bacc.Bacc("TRN2", target_bir_lowering=False, num_devices=1)
    arrays, args = {}, []
    for name, a in lay.items():
        a = np.ascontiguousarray(a)
        arrays[name] = a
        args.append(nc.dram_tensor(name, a.shape, mybir.dt.from_np(a.dtype), kind="ExternalInput").ap())
    args.append(nc.dram_tensor("out", (NB, P, TB, H), F32, kind="ExternalOutput").ap())
    build(nc, *args)
    r = run(nc, [arrays], core_ids=[0])
    return r.results[0]["out"].transpose(0, 2, 1, 3).reshape(NB, L, H)
```

```python
from contextlib import ExitStack

import concourse.bass as bass
from concourse import mybir

F32 = mybir.dt.float32
F32R = mybir.dt.float32r
U32 = mybir.dt.uint32
I32 = mybir.dt.int32
ALU = mybir.AluOpType
ACT = mybir.ActivationFunctionType

P = 128
NB, L, H = 4, 512, 512
DI, NS, R = 1024, 16, 32
TB = L // P
KH = H // P
DT = DI // P
SF = R + 2 * NS
TAPS = 4
INTER = 1376
FT = -(-INTER // P)
FL = INTER - (FT - 1) * P
GRP = 128
NG, NGD = H // GRP, INTER // GRP
LN_EPS, RMS_EPS = 1e-5, 1e-6
QC = 8
PAIRS = -(-FT // 2)
PC = 4 * P
QROWS = (NG * 2 * INTER + NGD * H) // P


def rows(ft):
    return P if ft < FT - 1 else FL


def products(pe, out, hi_l, lo_l, hi_r, lo_r, start, stop, **kw):
    pe.matmul(out, hi_l, hi_r, start=start, stop=False, **kw)
    pe.matmul(out, hi_l, lo_r, start=False, stop=False, **kw)
    return pe.matmul(out, lo_l, hi_r, start=False, stop=stop, **kw)


def build(nc, x, w_in, conv_w, conv_b, w_x, w_dt, a_log, d_skip, group_mean, w_out,
          qw_gu, qw_d, zeros, scales, g_idx, out):
    u_d = nc.dram_tensor("u_scratch", (NB, DT, P, L), F32, kind="Internal").ap()
    g_d = nc.dram_tensor("gate_scratch", (NB, DT, P, L), F32, kind="Internal").ap()
    bc_d = nc.dram_tensor("bc_scratch", (NB, 2 * NS, L), F32, kind="Internal").ap()
    x1_d = nc.dram_tensor("x1_scratch", (NB, P, TB, H), F32, kind="Internal").ap()
    ts_d = nc.dram_tensor("ts_scratch", (NB, R, 2, L), F32, kind="Internal").ap()

    hot_d = nc.dram_tensor("hot_scratch", (NGD, H + INTER), F32, kind="Internal").ap()
    rows_d = nc.dram_tensor("rows_scratch", (3, QROWS * P), F32, kind="Internal").ap()

    whole = ExitStack()
    with whole:
        def tensors(ctx):
            def sb(name, shape, dt=F32):
                return ctx.enter_context(nc.sbuf_tensor(name, shape, dt))

            def ps(name, shape):
                return ctx.enter_context(nc.psum_tensor(name, shape, F32))

            def sem(name):
                return ctx.enter_context(nc.semaphore(name))
            return sb, ps, sem

        sb, ps, sem = tensors(whole)
        ident = sb("ident", [P, P])
        a_neg = sb("a_neg", [P, DT, NS])
        dsk = sb("dsk", [P, DT])
        with ExitStack() as c:
            sbo, _, _ = tensors(c)
            wdt_hi, wdt_lo = sbo("wdt_hi", [R + 1, DI], F32R), sbo("wdt_lo", [R + 1, DI], F32R)
            ts_hl = sbo("ts_hl", [R + 1, 2, L], F32R)
            project(nc, tensors, wdt_hi, wdt_lo, ts_hl, ident, a_neg, dsk, x, w_in, conv_w, conv_b, w_x, w_dt,
                    a_log, d_skip, group_mean, zeros, scales, g_idx, u_d, g_d, bc_d, ts_d, hot_d, rows_d)
            scan(nc, tensors, ident, a_neg, dsk, wdt_hi, wdt_lo, ts_hl, x, w_out, u_d, g_d, bc_d, ts_d, x1_d)
        ffn(nc, tensors, x1_d, hot_d, rows_d, ident, qw_gu, qw_d, out)


def project(nc, tensors, wdt_hi, wdt_lo, ts_hl, ident, a_neg, dsk, x, w_in, conv_w, conv_b, w_x, w_dt,
            a_log, d_skip, group_mean, zeros, scales, g_idx, u_d, g_d, bc_d, ts_d, hot_d, rows_d):
    NR = 3
    with ExitStack() as c:
        sb, ps, sem = tensors(c)
        wraw = sb("wraw", [P, DT, 2 * KH * P])
        win_hi, win_lo = sb("win_hi", [P, DT, 2 * KH * P], F32R), sb("win_lo", [P, DT, 2 * KH * P], F32R)
        wxraw = sb("wxraw", [P, DT, SF])
        wx_hi, wx_lo = sb("wx_hi", [P, DT, SF], F32R), sb("wx_lo", [P, DT, SF], F32R)
        wdraw = sb("wdraw", [R + 1, DI])
        gmean = sb("gmean", [SF, P])
        eps = sb("eps", [SF, 1])
        cw, cb = sb("cw", [P, DT, TAPS]), sb("cb", [P, DT])
        stats, mv = sb("stats", [P, TB, 6]), sb("mv", [P, TB, 2])
        var_e, std, rstd = sb("var_e", [P, TB]), sb("std", [P, TB]), sb("rstd", [P, TB])
        xn = sb("xn", [P, TB, H])
        xt_hi, xt_lo = sb("xt_hi", [P, KH, L], F32R), sb("xt_lo", [P, KH, L], F32R)
        xc = sb("xc", [P, 2, L])
        u = sb("u", [P, 2, L])
        u_hi, u_lo = sb("u_hi", [P, 2, L], F32R), sb("u_lo", [P, 2, L], F32R)
        g = sb("g", [P, 2, L])
        feat, fsq, rms, rinv, fn = (sb(n, [SF, L]) for n in ("feat", "fsq", "rms", "rinv", "fn"))
        tsp = sb("ts_split", [R, 2, L], F32R)
        gi = sb("gi", [NGD, H + INTER], I32)
        hot = sb("hot", [NGD, H + INTER])
        hot_r = sb("hot_r", [NGD, H + INTER], F32R)
        pid, pidf = sb("pid", [P, 1], U32), sb("pidf", [P, 1])
        zw, zn = sb("zero_words", [QROWS, P // QC], U32), sb("zero_nibbles", [QROWS, P], U32)
        zr = sb("zero_rows", [QROWS, P], F32R)
        sf = sb("scale_rows", [QROWS, P])
        s_hi, s_lo = sb("scale_hi", [QROWS, P], F32R), sb("scale_lo", [QROWS, P], F32R)
        tp = [ps(f"tp{i}", [P, L]) for i in range(KH)]
        ip = [ps(f"ip{i}", [P, L]) for i in range(NR)]
        fp = ps("fp", [SF, L])
        ms = tp[KH - 1][0:SF, :]

        w_in_s = [sem(f"w_in{m}") for m in range(DT)]
        small_in, x_in = sem("small_in"), sem("x_in")
        w_split, w_rest = sem("w_split"), sem("w_rest")
        wx_split, wx_rest = sem("wx_split"), sem("wx_rest")
        ones_done, eps_done = sem("ones_done"), sem("eps_done")
        id_zero, id_done = sem("id_zero"), sem("id_done")
        st_done, mv_done, ve_done = sem("st_done"), sem("mv_done"), sem("ve_done")
        std_done, rstd_done, xn_done = sem("std_done"), sem("rstd_done"), sem("xn_done")
        tp_done = sem("tp_done")
        hi_done, lo_done = sem("hi_done"), sem("lo_done")
        ip_done = sem("ip_done")
        xc_first = sem("xc_first")
        tap_step, taps_done = sem("tap_step"), sem("taps_done")
        u_done, uhi_done, ulo_done = sem("u_done"), sem("uhi_done"), sem("ulo_done")
        g_done = sem("g_done")
        wx_used = sem("wx_used")
        u_out = [sem(f"u_out{i}") for i in range(2)]
        g_out = [sem(f"g_out{i}") for i in range(2)]
        feat_done, sq_done, ms_done, rms_done = sem("feat_done"), sem("sq_done"), sem("ms_done"), sem("rms_done")
        rinv_done, fn_done = sem("rinv_done"), sem("fn_done")
        tshi_done, tslo_done = sem("tshi_done"), sem("tslo_done")
        feat_out = sem("feat_out")
        quant_in, pid_done, pidf_done = sem("quant_in"), sem("pid_done"), sem("pidf_done")
        hot_step, hot_done = sem("hot_step"), sem("hot_done")
        nibble_done, zero_done = sem("nibble_done"), sem("zero_done")
        scale_hi_done, scale_lo_done, quant_out = sem("scale_hi_done"), sem("scale_lo_done"), sem("quant_out")

        def batches(body):
            def run(eng):
                body(0, True, False)
                with eng.Fori(1, NB - 1) as b:
                    body(b, False, False)
                body(NB - 1, False, True)
            return run

        with nc.Block() as block:
            @block.sync
            def _(sp):
                def load_x(b):
                    sp.dma_start(xn[:, :, :], x[bass.ds(b, 1)].rearrange("o p t h -> (o p) t h")).then_inc(x_in, 16)

                load_x(0)
                sp.dma_start(wraw[:, 0, :], w_in[:, 0, :]).then_inc(w_in_s[0], 16)
                for dst, src in ((wxraw[:, :, :], w_x), (wdraw[:, :], w_dt), (a_neg[:, :, :], a_log),
                                 (dsk[:, :], d_skip), (cw[:, :, :], conv_w), (cb[:, :], conv_b),
                                 (gmean[:, :], group_mean)):
                    sp.dma_start(dst, src).then_inc(small_in, 16)
                for m in range(1, DT):
                    sp.dma_start(wraw[:, m, :], w_in[:, m, :]).then_inc(w_in_s[m], 16)

                def store_features(b):
                    sp.wait_ge(fn_done, b)
                    sp.dma_start(bc_d[bass.ds(b - 1, 1)].rearrange("o n l -> (o n) l"),
                                 fn[R:SF, :]).then_inc(feat_out, 16)
                    sp.wait_ge(tslo_done, b)
                    sp.dma_start(ts_d[bass.ds(b - 1, 1)].rearrange("o r s l -> (o r) s l"),
                                 tsp[:, :, :].bitcast(F32)).then_inc(feat_out, 16)

                def body(b, first, last):
                    if not last:
                        sp.wait_ge(tp_done, b * KH + KH)
                        load_x(b + 1)
                    for m in range(DT):
                        for done, dst, src, out in ((u_done, u_d, u, u_out), (g_done, g_d, g, g_out)):
                            sp.wait_ge(done, b * DT + (m + 1))
                            sp.dma_start(dst[bass.ds(b, 1), m].rearrange("o p l -> (o p) l"),
                                         src[:, m % 2, :]).then_inc(out[m % 2], 16)
                        if m == 4 and not first:
                            store_features(b)

                for dst, src in ((zw, zeros), (sf, scales), (gi, g_idx.broadcast_to([NGD, H + INTER]))):
                    sp.dma_start(dst[:, :], src).then_inc(quant_in, 16)
                batches(body)(sp)
                for done, n, dst, src in ((zero_done, 1, rows_d[0], zr), (scale_hi_done, 1, rows_d[1], s_hi),
                                          (scale_lo_done, 1, rows_d[2], s_lo)):
                    sp.wait_ge(done, n)
                    sp.dma_start(dst.rearrange("(p c) -> p c", c=P),
                                 src[:, :].bitcast(F32)).then_inc(quant_out, 16)
                sp.wait_ge(hot_done, 1)
                sp.dma_start(hot_d, hot_r[:, :].bitcast(F32)).then_inc(quant_out, 16)
                store_features(NB)
                sp.wait_ge(quant_out, 16 * 4)
                for done in (*u_out, *g_out):
                    sp.wait_ge(done, 16 * NB * DT // 2)
                sp.wait_ge(feat_out, 1 + 32 * NB)

            @block.tensor
            def _(pe):
                def transposes(b):
                    for k in range(KH):
                        for t in range(TB):
                            if k == 0:
                                pe.wait_ge(xn_done, b * TB + (t + 1))
                            last = pe.transpose(tp[k][:, P * t:P * (t + 1)], xn[:, t, P * k:P * (k + 1)],
                                                ident[:, :])
                        last.then_inc(tp_done, 1)

                def features(b, m):
                    pe.wait_ge(uhi_done, b * DT + (m + 1))
                    pe.wait_ge(ulo_done, b * DT + (m + 1))
                    products(pe, fp[:, :], wx_hi[:, m, :], wx_lo[:, m, :], u_hi[:, m % 2, :], u_lo[:, m % 2, :],
                             start=(m == 0), stop=(m == DT - 1)).then_inc(wx_used, 1)

                def mean_squares(b):
                    pe.wait_ge(sq_done, b)
                    pe.matmul(tp[KH - 1][:, :], gmean[:, :], fsq[:, :], start=True, stop=True).then_inc(ms_done, 1)

                def body(b, first, last):
                    for j in range(2 * DT):
                        m, gate = j // 2, j % 2
                        if first and not gate:
                            pe.wait_ge(w_rest, m + 1)
                        if j >= NR or not first:
                            jj = j - NR if j >= NR else (2 * DT - 1, 2 * DT - 3, 2 * DT - 2)[j] - 2 * DT
                            pe.wait_ge(g_done if jj % 2 else taps_done, b * DT + (jj // 2 + 1))
                        for k in range(KH):
                            if j == 0:
                                pe.wait_ge(hi_done, b * KH + (k + 1))
                                pe.wait_ge(lo_done, b * KH + (k + 1))
                            s = slice((gate * KH + k) * P, (gate * KH + k + 1) * P)
                            last_mm = products(pe, ip[j % NR][:, :], win_hi[:, m, s], win_lo[:, m, s],
                                               xt_hi[:, k, :], xt_lo[:, k, :], start=(k == 0),
                                               stop=(k == KH - 1))
                        last_mm.then_inc(ip_done, 1)
                        if j == 1 and not first:
                            mean_squares(b)
                        if gate and m >= 1:
                            if m == 1 and first:
                                pe.wait_ge(wx_rest, 2)
                            if m == 1 and not first:
                                pe.wait_ge(feat_done, b)
                            features(b, m - 1)
                    if not last:
                        if not first:
                            pe.wait_ge(rms_done, b)
                        transposes(b + 1)
                    features(b, DT - 1)

                pe.wait_ge(id_done, 1)
                transposes(0)
                batches(body)(pe)
                mean_squares(NB)

            @block.scalar
            def _(act):
                def split_w(m):
                    act.wait_ge(w_in_s[m], 16)
                    act.activation(win_hi[:, m, :], wraw[:, m, :], ACT.Copy).then_inc(w_split, 1)

                def std_of(b):
                    act.wait_ge(ve_done, b + 1)
                    act.activation(std[:, :], var_e[:, :], ACT.Sqrt).then_inc(std_done, 1)

                def split_x(b):
                    for k in range(KH):
                        act.wait_ge(tp_done, b * KH + (k + 1))
                        if k == 0 and not (isinstance(b, int) and b == 0):
                            act.wait_ge(ip_done, b * 2 * DT)
                        act.activation(xt_hi[:, k, :], tp[k][:, :], ACT.Copy).then_inc(hi_done, 1)

                def norm_features(b):
                    act.wait_ge(ms_done, b)
                    act.activation(rms[:, :], ms, ACT.Sqrt, bias=eps[:, 0:1]).then_inc(rms_done, 1)

                def split_ts(b):
                    act.wait_ge(fn_done, b)
                    act.activation(tsp[:, 0, :], fn[0:R, :], ACT.Copy).then_inc(tshi_done, 1)

                def body(b, first, last):
                    for m in range(DT):
                        if first and m + 2 < DT:
                            split_w(m + 2)
                        act.wait_ge(ip_done, b * 2 * DT + (2 * m + 1))
                        if m >= 2 or not first:
                            act.wait_ge(u_done, b * DT + (m - 1))
                        act.activation(xc[:, m % 2, :], ip[(2 * m) % NR][:, :], ACT.Identity,
                                       bias=cb[:, m:m + 1], scale=cw[:, m, TAPS - 1:TAPS]).then_inc(xc_first, 1)
                        act.wait_ge(ip_done, b * 2 * DT + (2 * m + 2))
                        if m >= 2 or not first:
                            act.wait_ge(g_out[m % 2], b * (8 * DT) + 16 * (m // 2))
                        act.activation(g[:, m % 2, :], ip[(2 * m + 1) % NR][:, :], ACT.Silu).then_inc(g_done, 1)
                        act.wait_ge(taps_done, b * DT + (m + 1))
                        if m >= 2 or not first:
                            act.wait_ge(u_out[m % 2], b * (8 * DT) + 16 * (m // 2))
                            act.wait_ge(ulo_done, b * DT + (m - 1))
                            act.wait_ge(wx_used, b * DT + (m - 1))
                        act.activation(u[:, m % 2, :], xc[:, m % 2, :], ACT.Silu).then_inc(u_done, 1)
                        act.wait_ge(u_done, b * DT + (m + 1))
                        act.activation(u_hi[:, m % 2, :], u[:, m % 2, :], ACT.Copy).then_inc(uhi_done, 1)
                        if m == 1 and not first:
                            norm_features(b)
                        if m == 2 and not first:
                            split_ts(b)
                        if m == 4 and not last:
                            std_of(b + 1)
                    if not last:
                        split_x(b + 1)
                    act.wait_ge(wx_used, b * DT + DT)
                    act.activation(feat[:, :], fp[:, :], ACT.Copy).then_inc(feat_done, 1)
                    act.wait_ge(feat_done, b + 1)
                    act.activation(fsq[:, :], feat[:, :], ACT.Square).then_inc(sq_done, 1)

                split_w(0)
                std_of(0)
                split_w(1)
                act.wait_ge(small_in, 16 * 7)
                act.activation(wx_hi[:, :, :], wxraw[:, :, :], ACT.Copy).then_inc(wx_split, 1)
                act.activation(wdt_hi[:, :], wdraw[:, :], ACT.Copy).then_inc(wx_split, 1)
                split_x(0)
                act.wait_ge(eps_done, 1)
                batches(body)(act)
                norm_features(NB)
                split_ts(NB)

            @block.vector
            def _(dve):
                def rest_w(m):
                    dve.wait_ge(w_split, m + 1)
                    dve.tensor_tensor(win_lo[:, m, :], wraw[:, m, :], win_hi[:, m, :].bitcast(F32),
                                      ALU.subtract).then_inc(w_rest, 1)

                def norm_stats(b):
                    dve.wait_ge(x_in, b * 16 + 16)
                    for t in range(TB):
                        dve.bn_stats(stats[:, t, :], xn[:, t, :]).then_inc(st_done, 1)

                def norm_mean(b):
                    for t in range(TB):
                        dve.bn_aggr(mv[:, t, :], stats[:, t, :]).then_inc(mv_done, 1)

                def norm_var(b):
                    dve.wait_ge(mv_done, b * TB + TB)
                    dve.tensor_scalar(var_e[:, :], mv[:, :, 1], LN_EPS, None, ALU.add).then_inc(ve_done, 1)

                def norm_apply(b):
                    dve.wait_ge(std_done, b + 1)
                    dve.reciprocal(rstd[:, :], std[:, :]).then_inc(rstd_done, 1)
                    dve.wait_ge(rstd_done, b + 1)
                    for t in range(TB):
                        dve.tensor_scalar(xn[:, t, :], xn[:, t, :], mv[:, t, 0:1], rstd[:, t:t + 1],
                                          ALU.subtract, ALU.mult).then_inc(xn_done, 1)

                def rest_x(b):
                    for k in range(KH):
                        dve.wait_ge(hi_done, b * KH + (k + 1))
                        dve.tensor_tensor(xt_lo[:, k, :], tp[k][:, :], xt_hi[:, k, :].bitcast(F32),
                                          ALU.subtract).then_inc(lo_done, 1)

                def norm_features(b):
                    dve.wait_ge(rms_done, b)
                    dve.reciprocal(rinv[:, :], rms[:, :]).then_inc(rinv_done, 1)
                    dve.wait_ge(rinv_done, b)
                    dve.wait_ge(feat_out, (b - 1) * 32 + 1)
                    dve.tensor_tensor(fn[:, :], feat[:, :], rinv[:, :], ALU.mult).then_inc(fn_done, 1)

                def rest_ts(b):
                    dve.wait_ge(tshi_done, b)
                    dve.tensor_tensor(tsp[:, 1, :], fn[0:R, :], tsp[:, 0, :].bitcast(F32),
                                      ALU.subtract).then_inc(tslo_done, 1)

                def zero_rows():
                    dve.wait_ge(quant_in, 16 * 3)
                    for j in range(QC):
                        dve.tensor_scalar(zn[:, :].rearrange("g (c j) -> g c j", j=QC)[:, :, j], zw[:, :], 4 * j,
                                          15, ALU.logical_shift_right, ALU.bitwise_and).then_inc(nibble_done, 1)
                    dve.wait_ge(nibble_done, QC)
                    dve.tensor_scalar(zr[:, :], zn[:, :], 1.0, None, ALU.add).then_inc(zero_done, 1)

                def scale_rows():
                    dve.tensor_copy(s_hi[:, :], sf[:, :]).then_inc(scale_hi_done, 1)
                    dve.wait_ge(scale_hi_done, 1)
                    dve.tensor_tensor(s_lo[:, :], sf[:, :], s_hi[:, :].bitcast(F32),
                                      ALU.subtract).then_inc(scale_lo_done, 1)

                parts = ((slice(0, H), NG), (slice(H, H + INTER), NGD))

                def wrap_index():
                    wrap = gi[:, :].bitcast(F32)
                    dve.tensor_copy(hot[:, :], gi[:, :]).then_inc(hot_step, 1)
                    dve.wait_ge(hot_step, 1)
                    for s, n in parts:
                        dve.tensor_scalar(wrap[:, s], hot[:, s], 0.0, float(n), ALU.is_lt,
                                          ALU.mult).then_inc(hot_step, 1)
                    dve.wait_ge(hot_step, 3)
                    dve.tensor_tensor(hot[:, :], hot[:, :], wrap, ALU.add).then_inc(hot_step, 1)

                def clamp_index():
                    dve.wait_ge(hot_step, 4)
                    for s, n in parts:
                        dve.tensor_scalar(hot[:, s], hot[:, s], 0.0, float(n - 1), ALU.max,
                                          ALU.min).then_inc(hot_step, 1)

                def one_hot():
                    dve.wait_ge(hot_step, 6)
                    dve.wait_ge(pidf_done, 1)
                    dve.tensor_scalar(hot[:, :], hot[:, :], pidf[0:NGD, 0:1], None,
                                      ALU.is_equal).then_inc(hot_step, 1)
                    dve.wait_ge(hot_step, 7)
                    dve.tensor_copy(hot_r[:, :], hot[:, :]).then_inc(hot_done, 1)

                def body(b, first, last):
                    for m in range(DT):
                        if first and m + 2 < DT:
                            rest_w(m + 2)
                        if m == 2 and not last:
                            dve.wait_ge(st_done, (b + 1) * TB + TB)
                        for j in range(TAPS - 1):
                            s = TAPS - 1 - j
                            if j == 0:
                                dve.wait_ge(xc_first, b * DT + (m + 1))
                            else:
                                dve.wait_ge(tap_step, b * DT * (TAPS - 2) + (m * (TAPS - 2) + j))
                            dve.scalar_tensor_tensor(
                                out=xc[:, m % 2, s:], in0=ip[(2 * m) % NR][:, 0:L - s],
                                scalar=cw[:, m, j:j + 1], in1=xc[:, m % 2, s:], op0=ALU.mult,
                                op1=ALU.add).then_inc(taps_done if j == TAPS - 2 else tap_step, 1)
                        if not last:
                            if m == 1:
                                norm_stats(b + 1)
                            if m == 2:
                                norm_mean(b + 1)
                            if m == 3:
                                norm_var(b + 1)
                            if m == 5:
                                norm_apply(b + 1)
                        if not first:
                            if m == 1:
                                norm_features(b)
                            if m == 3:
                                rest_ts(b)
                        if last:
                            if m == 2:
                                zero_rows()
                                scale_rows()
                            if m == 4:
                                wrap_index()
                            if m == 5:
                                clamp_index()
                            if m == 6:
                                one_hot()
                    if not last:
                        rest_x(b + 1)

                dve.memset(eps[:, :], RMS_EPS).then_inc(eps_done, 1)
                dve.wait_ge(eps_done, 1)
                dve.memset(fn[0:1, 0:1], 0.0).then_inc(feat_out, 1)
                dve.wait_ge(pid_done, 1)
                dve.tensor_copy(pidf[:, :], pid[:, :]).then_inc(pidf_done, 1)
                dve.memset(ts_hl[R:R + 1, 0, :].bitcast(F32), 1.0).then_inc(ones_done, 1)
                dve.memset(ts_hl[R:R + 1, 1, :].bitcast(F32), 0.0).then_inc(ones_done, 1)
                norm_stats(0)
                dve.wait_ge(st_done, TB)
                norm_mean(0)
                norm_var(0)
                rest_w(0)
                norm_apply(0)
                rest_w(1)
                rest_x(0)
                dve.wait_ge(wx_split, 2)
                dve.tensor_tensor(wx_lo[:, :, :], wxraw[:, :, :], wx_hi[:, :, :].bitcast(F32),
                                  ALU.subtract).then_inc(wx_rest, 1)
                dve.tensor_tensor(wdt_lo[:, :], wdraw[:, :], wdt_hi[:, :].bitcast(F32),
                                  ALU.subtract).then_inc(wx_rest, 1)
                batches(body)(dve)
                norm_features(NB)
                rest_ts(NB)

            @block.gpsimd
            def _(pool):
                pool.iota(pid[:, :], pattern=[[0, 1]], base=0, channel_multiplier=1).then_inc(pid_done, 1)
                pool.memset(ident[:, :], 0.0).then_inc(id_zero, 1)
                pool.wait_ge(id_zero, 1)
                pool.affine_select(out=ident[:, :], in_=ident[:, :], compare_op=ALU.not_equal, fill=1.0,
                                   base=0, pattern=[[-1, P]], channel_multiplier=1).then_inc(id_done, 1)

                def body(b, first, last):
                    for m in range(DT):
                        pool.wait_ge(uhi_done, b * DT + (m + 1))
                        pool.tensor_tensor(u_lo[:, m % 2, :], u[:, m % 2, :],
                                           u_hi[:, m % 2, :].bitcast(F32), ALU.subtract).then_inc(ulo_done, 1)

                batches(body)(pool)


def scan(nc, tensors, ident, a_neg, dsk, wdt_hi, wdt_lo, ts_hl, x, w_out, u_d, g_d, bc_d, ts_d, x1_d):
    RA, RW, NQ = 4, 8, 4
    NI = NS // 2
    AT_EXP, AT_LN, AT_SUM, AT_GAIN, AT_DT, AT_OUT = 2, 4, 5, 7, 6, 3
    UNITS = DT * NI
    NL = NS // NQ
    with ExitStack() as c:
        sb, ps, sem = tensors(c)
        wo = sb("wo", [P, DT, H])
        bb, cc = sb("bb", [P, NS, L]), sb("cc", [P, NS, L])
        u, g = sb("u_s", [P, 2, L]), sb("g_s", [P, 2, L])
        dt, dtu = sb("dt", [P, 2, L]), sb("dtu", [P, 2, L])
        sp1, sp2 = sb("sp1", [P, L]), sb("sp2", [P, L])
        decay = sb("decay", [P, RA, 2, L])
        work = sb("work", [P, RW, 2, L])
        yg = sb("yg", [P, 2, L])
        one = sb("one", [P, 1])
        xr = sb("xr", [P, TB, H])
        d_diag = sb("d_diag", [P, DT, P])
        dtp = ps("dtp", [P, L])
        yp = [ps(f"yp{i}", [P, L]) for i in range(2)]
        op = [ps(f"op{t}", [P, H]) for t in range(TB)]

        wo_in, diag_done, one_done = sem("wo_in"), sem("diag_done"), sem("one_done")
        bb_in = [sem(f"bb_in{q}") for q in range(NQ)]
        cc_in = [sem(f"cc_in{q}") for q in range(NQ)]
        u_in = [sem(f"u_in{i}") for i in range(2)]
        g_in = [sem(f"g_in{i}") for i in range(2)]
        ts_in = sem("ts_in")
        dtp_done = sem("dtp_done")
        abs_done, e_done, w_done, ln_done = sem("abs_done"), sem("e_done"), sem("w_done"), sem("ln_done")
        round_done, log_done = sem("round_done"), sem("log_done")
        dt_done, dtu_done = sem("dt_done"), sem("dtu_done")
        decay_done, drive_done = sem("decay_done"), sem("drive_done")
        h_done, prod_done = sem("h_done"), sem("prod_done")
        unit_summed = sem("unit_summed")
        y_done = sem("y_done")
        yg_done = sem("yg_done")
        a_exp, a_done = sem("a_exp"), sem("a_done")
        op_done, res_done = sem("op_done"), sem("res_done")

        x_in, x1_out = sem("xr_in"), sem("x1_out")
        reset_done = sem("reset_done")

        def batches(eng, body):
            body(0, True, False)
            with eng.Fori(1, NB - 1) as b:
                body(b, False, False)
            body(NB - 1, False, True)

        with nc.Block() as block:
            @block.sync
            def _(sp):
                def load_ts(b):
                    sp.dma_start(ts_hl[0:R, :, :].bitcast(F32), ts_d[bass.ds(b, 1)].rearrange(
                        "o r s l -> (o r) s l")).then_inc(ts_in, 16)

                def load_bc(b, q):
                    s = slice(q * NL, (q + 1) * NL)
                    for dst, off, done in ((bb, 0, bb_in), (cc, NS, cc_in)):
                        src = bc_d[bass.ds(b, 1), off + s.start:off + s.stop].rearrange(
                            "o n l -> o (n l)").broadcast_to([P, NL * L])
                        sp.dma_start(dst[:, s, :].rearrange("p n l -> p (n l)"), src).then_inc(done[q], 16)

                def load_ug(b, d):
                    for dst, src, done in ((u, u_d, u_in), (g, g_d, g_in)):
                        sp.dma_start(dst[:, d % 2, :], src[bass.ds(b, 1), d].rearrange(
                            "o p l -> (o p) l")).then_inc(done[d % 2], 16)

                def load_x(b):
                    sp.dma_start(xr[:, :, :], x[bass.ds(b, 1)].rearrange("o p t h -> (o p) t h")).then_inc(x_in, 16)

                def store_x1(b):
                    sp.wait_ge(res_done, b * TB)
                    sp.dma_start(x1_d[bass.ds(b - 1, 1)].rearrange("o p t h -> (o p) t h"),
                                 xr[:, :, :]).then_inc(x1_out, 16)

                load_ts(0)
                load_ug(0, 0)
                for q in range(NQ):
                    load_bc(0, q)
                load_ug(0, 1)
                sp.dma_start(wo[:, :, :], w_out).then_inc(wo_in, 16)
                load_x(0)

                def body(b, first, last):
                    for d in range(1 if not first else 2, DT):
                        sp.wait_ge(yg_done, b * DT + (d - 1))
                        load_ug(b, d)
                        if d == 3 and not first:
                            store_x1(b)
                            sp.wait_ge(x1_out, b * 16)
                            load_x(b)
                    if last:
                        store_x1(NB)
                        sp.wait_ge(x1_out, NB * 16)
                        return
                    sp.wait_ge(dtp_done, b * DT + DT)
                    load_ts(b + 1)
                    sp.wait_ge(yg_done, b * DT + (DT - 1))
                    load_ug(b + 1, 0)
                    for q in range(NQ):
                        sp.wait_ge(prod_done, b * UNITS + (UNITS - NI + (q + 1) * NI // NQ))
                        load_bc(b + 1, q)

                batches(sp, body)

            @block.tensor
            def _(pe):
                def dt_product(b, d):
                    if d == 0:
                        pe.wait_ge(ts_in, b * 16 + 16)
                    s = slice(P * d, P * (d + 1))
                    products(pe, dtp[:, :], wdt_hi[:, s], wdt_lo[:, s], ts_hl[:, 0, :],
                             ts_hl[:, 1, :], start=True, stop=True).then_inc(dtp_done, 1)

                def out_product(b, d):
                    pe.wait_ge(yg_done, b * DT + (d + 1))
                    for t in range(TB):
                        s = slice(P * t, P * (t + 1))
                        last = pe.matmul(op[t][:, :], yg[:, d % 2, s], wo[:, d % DT, :], start=(d == 0),
                                         stop=(d % DT == DT - 1))
                    last.then_inc(op_done, 1)

                def body(b, first, last):
                    for d in range(DT):
                        for i in range(NI):
                            k = d * NI + i
                            pe.wait_ge(prod_done, b * UNITS + (k + 1))
                            if i == 0 and (d >= 2 or not first):
                                pe.wait_ge(yg_done, b * DT + (d - 1))
                            pe.matmul(yp[d % 2][:, :], ident[:, :], work[:, k % RW, 0, :],
                                      start=(i == 0), stop=False)
                            pe.matmul(yp[d % 2][:, :], ident[:, :], work[:, k % RW, 1, :],
                                      start=False, stop=False).then_inc(unit_summed, 1)
                            if i == AT_DT and not (last and d >= DT - 2):
                                pe.wait_ge(dt_done, b * DT + (d + 2))
                                dt_product(*((b, d + 2) if d + 2 < DT else (b + 1, d + 2 - DT)))
                            if i == AT_OUT and not (first and d == 0):
                                if d == 0:
                                    out_product(b, -1)
                                else:
                                    if d == 1 and first:
                                        pe.wait_ge(wo_in, 16)
                                    if d == 1 and not first:
                                        pe.wait_ge(res_done, b * TB)
                                    out_product(b, d - 1)
                        pe.wait_ge(u_in[d % 2], b * (8 * DT) + 16 * (d // 2 + 1))
                        if d == 0 and first:
                            pe.wait_ge(diag_done, DT)
                        pe.matmul(yp[d % 2][:, :], d_diag[:, d, :], u[:, d % 2, :], start=False,
                                  stop=True).then_inc(y_done, 1)
                    if last:
                        out_product(b, DT - 1)

                dt_product(0, 0)
                pe.wait_ge(dt_done, 1)
                dt_product(0, 1)
                batches(pe, body)

            @block.scalar
            def _(act):
                act.preload_act_table_set("natural_log_exp_and_others")
                act.activation(a_neg[:, :, :], a_neg[:, :, :], ACT.Exp).then_inc(a_exp, 1)
                act.wait_ge(a_exp, 1)
                act.activation(a_neg[:, :, :], a_neg[:, :, :], ACT.Copy, scale=-1.0).then_inc(a_done, 1)
                def softplus_exp(b, d):
                    act.wait_ge(dtp_done, b * DT + (d + 1))
                    act.activation(sp1[:, :], dtp[:, :], ACT.Abs).then_inc(abs_done, 1)
                    act.wait_ge(abs_done, b * DT + (d + 1))
                    act.activation(sp1[:, :], sp1[:, :], ACT.Exp, scale=-1.0).then_inc(e_done, 1)
                    act.wait_ge(e_done, b * DT + (d + 1))
                    act.activation(sp2[:, :], sp1[:, :], ACT.Identity, bias=one[:, 0:1]).then_inc(w_done, 1)

                def softplus_log(b, d):
                    act.wait_ge(round_done, b * DT + (d + 1))
                    act.activation(sp2[:, :], sp2[:, :], ACT.Ln).then_inc(ln_done, 1)

                def body(b, first, last):
                    for d in range(DT):
                        ahead = (b, d + 1) if d + 1 < DT else (b + 1, 0)
                        more = d + 1 < DT or not last
                        act.wait_ge(dt_done, b * DT + (d + 1))
                        for i in range(NI):
                            k = d * NI + i
                            if not first or k >= RA:
                                act.wait_ge(h_done, b * UNITS + (k - RA + 1))
                            for m in range(2):
                                n = 2 * i + m
                                done = act.activation(decay[:, k % RA, m, 1:], dt[:, d % 2, 1:], ACT.Exp,
                                                      scale=a_neg[:, d, n:n + 1])
                            done.then_inc(decay_done, 1)
                            if i == AT_EXP and more:
                                softplus_exp(*ahead)
                            if i == AT_LN and more:
                                softplus_log(*ahead)
                            if i == NI - 1 and first and d == 0:
                                for m in range(DT):
                                    act.activation(d_diag[:, m, :], ident[:, :], ACT.Identity,
                                                   scale=dsk[:, m:m + 1]).then_inc(diag_done, 1)

                act.wait_ge(one_done, 1)
                softplus_exp(0, 0)
                softplus_log(0, 0)
                act.wait_ge(a_done, 1)
                batches(act, body)

            @block.vector
            def _(dve):
                def softplus_lost(b, d):
                    dve.wait_ge(w_done, b * DT + (d + 1))
                    dve.scalar_tensor_tensor(out=sp1[:, :], in0=sp2[:, :], scalar=-1.0, in1=sp1[:, :],
                                             op0=ALU.add, op1=ALU.subtract).then_inc(round_done, 1)

                def softplus_log(b, d):
                    dve.wait_ge(ln_done, b * DT + (d + 1))
                    dve.tensor_tensor(sp2[:, :], sp2[:, :], sp1[:, :], ALU.subtract).then_inc(log_done, 1)

                def softplus_sum(b, d):
                    dve.wait_ge(log_done, b * DT + (d + 1))
                    dve.scalar_tensor_tensor(out=dt[:, d % 2, :], in0=dtp[:, :], scalar=0.0,
                                             in1=sp2[:, :], op0=ALU.max, op1=ALU.add).then_inc(dt_done, 1)

                def gate_y(b, d):
                    dve.wait_ge(y_done, b * DT + (d + 1))
                    dve.wait_ge(g_in[d % 2], b * (8 * DT) + 16 * (d // 2 + 1))
                    if not isinstance(b, int) or b * DT + d >= 2:
                        dve.wait_ge(op_done, b * DT + (d - 1))
                    dve.tensor_tensor(yg[:, d % 2, :], yp[d % 2][:, :], g[:, d % 2, :], ALU.mult).then_inc(yg_done, 1)

                def scan_unit(b, k):
                    dve.wait_ge(decay_done, b * UNITS + (k + 1))
                    dve.wait_ge(drive_done, b * UNITS + (k + 1))
                    w = work[:, k % RW, :, :].rearrange("p m l -> p (m l)")
                    dve.tensor_tensor_scan(w, decay[:, k % RA, :, :].rearrange("p m l -> p (m l)"), w,
                                           0.0, ALU.mult, ALU.add).then_inc(h_done, 1)

                def read_unit(b, k):
                    if k in range(0, NI, NI // NQ):
                        dve.wait_ge(cc_in[k * NQ // NI], b * 16 + 16)
                    dve.wait_ge(h_done, b * UNITS + (k + 1))
                    n = 2 * (k % NI)
                    w = work[:, k % RW, :, :]
                    dve.tensor_tensor(w, w, cc[:, n:n + 2, :], ALU.mult).then_inc(prod_done, 1)

                def residual(b):
                    dve.wait_ge(op_done, b * DT)
                    dve.wait_ge(x_in, b * 16)
                    for t in range(TB):
                        dve.tensor_tensor(xr[:, t, :], op[t][:, :], xr[:, t, :], ALU.add).then_inc(res_done, 1)

                def body(b, first, last):
                    for k in range(UNITS):
                        d, i = divmod(k, NI)
                        ahead = (b, d + 1) if d + 1 < DT else (b + 1, 0)
                        more = d + 1 < DT or not last
                        scan_unit(b, k)
                        if k >= 1 or not first:
                            read_unit(b, k - 1)
                        if i == 2 and not (first and d == 0):
                            gate_y(b, d - 1)
                        if i == AT_EXP and more:
                            softplus_lost(*ahead)
                        if i == AT_SUM and more and d % 2:
                            softplus_log(*ahead)
                        if i == AT_SUM and more:
                            softplus_sum(*ahead)
                        if i == 1 and d == 1 and not first:
                            residual(b)
                    if last:
                        read_unit(b, UNITS - 1)
                        gate_y(b, DT - 1)
                        residual(NB)

                dve.memset(decay[:, :, :, 0:1], 0.0).then_inc(reset_done, 1)
                dve.memset(one[:, :], 1.0).then_inc(one_done, 1)
                dve.wait_ge(reset_done, 1)
                softplus_lost(0, 0)
                softplus_log(0, 0)
                softplus_sum(0, 0)
                batches(dve, body)

            @block.gpsimd
            def _(pool):
                def input_gain(b, d):
                    pool.wait_ge(dt_done, b * DT + (d + 1))
                    pool.wait_ge(u_in[d % 2], b * (8 * DT) + 16 * (d // 2 + 1))
                    pool.tensor_tensor(dtu[:, d % 2, :], dt[:, d % 2, :], u[:, d % 2, :],
                                       ALU.mult).then_inc(dtu_done, 1)

                def softplus_log(b, d):
                    pool.wait_ge(ln_done, b * DT + (d + 1))
                    pool.tensor_tensor(sp2[:, :], sp2[:, :], sp1[:, :], ALU.subtract).then_inc(log_done, 1)

                def body(b, first, last):
                    for k in range(UNITS):
                        d, i = divmod(k, NI)
                        ahead = (b, d + 1) if d + 1 < DT else (b + 1, 0)
                        more = d + 1 < DT or not last
                        if i == 0:
                            pool.wait_ge(dtu_done, b * DT + (d + 1))
                        if k in range(0, NI, NI // NQ):
                            pool.wait_ge(bb_in[k * NQ // NI], b * 16 + 16)
                        if k >= RW or not first:
                            pool.wait_ge(unit_summed, b * UNITS + (k - RW + 1))
                        n = 2 * i
                        pool.tensor_tensor(work[:, k % RW, :, :],
                                           dtu[:, d % 2:d % 2 + 1, :].broadcast_to([P, 2, L]),
                                           bb[:, n:n + 2, :], ALU.mult).then_inc(drive_done, 1)
                        if i == AT_SUM and more and d % 2 == 0:
                            softplus_log(*ahead)
                        if i == AT_GAIN and more:
                            input_gain(*ahead)

                input_gain(0, 0)
                batches(pool, body)


def ffn(nc, tensors, x1_d, hot_d, rows_d, ident, qw_gu, qw_d, out):
    RQ = 3
    with ExitStack() as c:
        sb, ps, sem = tensors(c)
        wg_hi, wg_lo = sb("wg_hi", [P, KH, 2 * INTER], F32R), sb("wg_lo", [P, KH, 2 * INTER], F32R)
        wd_hi, wd_lo = sb("wd_hi", [P, FT, H], F32R), sb("wd_lo", [P, FT, H], F32R)
        hot_gu, hot_dn = sb("hot_gu", [2 * NG, H], F32R), sb("hot_dn", [2 * NGD, INTER], F32R)
        zeros_gu, zeros_dn = sb("zeros_gu", [NG, 2, PC], F32R), sb("zeros_dn", [NGD, H], F32R)
        scales_gu, scales_dn = sb("scales_gu", [2 * NG, 2, PC], F32R), sb("scales_dn", [2 * NGD, H], F32R)
        q = sb("q", [P, RQ, PC], U32)
        pid, shift = sb("pid2", [P, 1], U32), sb("shift", [P, 1], U32)
        stats, mv = sb("stats2", [P, TB, 6]), sb("mv2", [P, TB, 2])
        var_e, std, rstd = sb("var_e2", [P, TB]), sb("std2", [P, TB]), sb("rstd2", [P, TB])
        xn = sb("xn2", [P, TB, H])
        xr = sb("xr2", [P, TB, H])
        xt_hi, xt_lo = sb("xt_hi2", [P, KH, L], F32R), sb("xt_lo2", [P, KH, L], F32R)
        sg, hf = sb("sg", [P, L]), sb("hf", [P, L])
        h_hi, h_lo = sb("h_hi", [P, 2, L], F32R), sb("h_lo", [P, 2, L], F32R)
        gp = [ps(f"gp{i}", [P, L]) for i in range(2)]
        up = [ps(f"up{i}", [P, L]) for i in range(2)]
        tp = [gp[1], up[1], gp[0], up[0]]
        dp = [ps(f"dp{t}", [P, H]) for t in range(TB)]

        hot_in, rows_dn_in = sem("hot_in"), sem("rows_dn_in")
        rows_in = [sem(f"rows_in{i}") for i in range(2)]
        q_in = [sem(f"q_in{i}") for i in range(RQ)]
        pid_done, shift_done = sem("pid2_done"), sem("shift_done")
        nib_done = sem("nib_done")
        picked = sem("picked")
        sub_done, weight_done = sem("sub_done"), sem("weight_done")
        whi_done, wlo_done = sem("whi_done"), sem("wlo_done")
        x_in, xr_in = sem("x1_in"), sem("xr1_in")
        st_done, mv_done, ve_done = sem("st2_done"), sem("mv2_done"), sem("ve2_done")
        std_done, rstd_done, xn_done = sem("std2_done"), sem("rstd2_done"), sem("xn2_done")
        tp_done, hi_done, lo_done = sem("tp2_done"), sem("hi2_done"), sem("lo2_done")
        gate_done, up_done = sem("gate_done"), sem("up_done")
        sg_done, hf_done, hhi_done, hlo_done = sem("sg_done"), sem("hf_done"), sem("hhi_done"), sem("hlo_done")
        dp_done, res_done, out_done = sem("dp_done"), sem("res2_done"), sem("out_done")

        units = []
        for p in range(PAIRS):
            units += [(False, k, PC * p, P, min(PC, 2 * INTER - PC * p)) for k in range(KH)]
            units += [(True, f, 0, rows(f), H) for f in range(2 * p, min(2 * p + 2, FT))]
        BEFORE = range(0, 5)
        UP = KH + 2

        def after(f, stage):
            if f == 0:
                return (range(5, 7), range(7, 9), range(0))[stage]
            i = 9 + 3 * (f - 1) + stage
            return range(i, min(i + 1, len(units)))

        def zero_scale_banks(i):
            if i < 9:
                return dp[2 * (i % 2)], dp[2 * (i % 2) + 1]
            return gp[1], up[1]

        def pair_units(p):
            return UP * p + KH

        def down_units(f):
            return UP * (f // 2) + KH + f % 2 + 1

        def columns(f):
            width = P if f < FT - 1 else FL
            s = PC * (f // 2) + width * (f % 2 if f < FT - 1 else 0)
            return s, s + (2 * P if f < FT - 1 else FL)

        def weights(of_gu, of_dn, i):
            down, tile, c0, kk, nn = units[i]
            return (of_dn if down else of_gu)[0:kk, tile, c0:c0 + nn]

        def batches(body):
            def run(eng):
                body(0, True, False)
                with eng.Fori(1, NB - 1) as b:
                    body(b, False, False)
                body(NB - 1, False, True)
            return run

        with nc.Block() as block:
            @block.sync
            def _(sp):
                def load_x(b, dst, done):
                    sp.dma_start(dst[:, :, :], x1_d[bass.ds(b, 1)].rearrange(
                        "o p t h -> (o p) t h")).then_inc(done, 16)

                def load_rows(p):
                    _, _, c0, _, nn = units[UP * p]
                    src = rows_d[:, 0:NG * 2 * INTER].rearrange("j (g n) -> j g n", g=NG)[:, :, c0:c0 + nn]
                    for dst, j in ((zeros_gu, 0), (scales_gu[0:NG], 1), (scales_gu[NG:2 * NG], 2)):
                        sp.dma_start(dst[:, p % 2, 0:nn].bitcast(F32), src[j]).then_inc(rows_in[p % 2], 16)

                def load_q(i):
                    down, tile, c0, kk, nn = units[i]
                    src = (qw_d if down else qw_gu)[P // QC * tile:P // QC * tile + kk // QC, c0:c0 + nn]
                    sp.dma_start(q[0:kk, i % RQ, 0:nn],
                                 src.unsqueeze(1).broadcast_to([kk // QC, QC, nn])).then_inc(q_in[i % RQ], 16)

                def body(b, first, last):
                    if first:
                        for i in range(RQ, len(units)):
                            if i % UP == 0 and i // UP + 1 < PAIRS:
                                p = i // UP + 1
                                sp.wait_ge(picked, pair_units(p - 2))
                                load_rows(p)
                            if i == 2 * RQ:
                                load_x(0, xr, xr_in)
                                sp.wait_ge(tp_done, KH)
                                load_x(1, xn, x_in)
                            sp.wait_ge(whi_done, i - RQ + 1)
                            sp.wait_ge(wlo_done, i - RQ + 1)
                            load_q(i)
                    else:
                        sp.wait_ge(out_done, b * 16)
                        load_x(b, xr, xr_in)
                        if not last:
                            sp.wait_ge(tp_done, b * KH + KH)
                            load_x(b + 1, xn, x_in)
                    sp.wait_ge(res_done, b * TB + TB)
                    sp.dma_start(out[bass.ds(b, 1)].rearrange("o p t h -> (o p) t h"),
                                 xr[:, :, :]).then_inc(out_done, 16)

                load_x(0, xn, x_in)
                load_rows(0)
                for i in range(2):
                    sp.dma_start(hot_gu[NG * i:NG * (i + 1), :].bitcast(F32), hot_d[0:NG, 0:H]).then_inc(hot_in, 16)
                for i in range(RQ):
                    load_q(i)
                for i in range(2):
                    sp.dma_start(hot_dn[NGD * i:NGD * (i + 1), :].bitcast(F32),
                                 hot_d[:, H:H + INTER]).then_inc(rows_dn_in, 16)
                src = rows_d[:, NG * 2 * INTER:].rearrange("j (g n) -> j g n", g=NGD)
                for dst, j in ((zeros_dn, 0), (scales_dn[0:NGD], 1), (scales_dn[NGD:2 * NGD], 2)):
                    sp.dma_start(dst[:, :].bitcast(F32), src[j]).then_inc(rows_dn_in, 16)
                load_rows(1)
                batches(body)(sp)
                sp.wait_ge(out_done, 16 * NB)

            @block.tensor
            def _(pe):
                def pick(i):
                    down, tile, c0, kk, nn = units[i]
                    if i == 0:
                        pe.wait_ge(hot_in, 32)
                    if down and tile == 0:
                        pe.wait_ge(rows_dn_in, 16 * 5)
                    if not down and tile == 0:
                        p = i // UP
                        pe.wait_ge(rows_in[p % 2], 48 * (p // 2 + 1))
                    if 2 <= i:
                        pe.wait_ge(weight_done, i - 1 if i < 9 else i)
                    z, s = zero_scale_banks(i)
                    cols = slice(P * tile, P * tile + kk)
                    if down:
                        hot, groups, zero, scale = hot_dn, NGD, zeros_dn, scales_dn
                    else:
                        slot = (i // UP) % 2
                        hot, groups, zero, scale = hot_gu, NG, zeros_gu[:, slot], scales_gu[:, slot]
                    pe.matmul(z[0:kk, 0:nn], hot[0:groups, cols], zero[:, 0:nn], start=True, stop=True)
                    pe.matmul(s[0:kk, 0:nn], hot[:, cols], scale[:, 0:nn], start=True,
                              stop=True).then_inc(picked, 1)

                def transposes(b, ks):
                    for k in ks:
                        for t in range(TB):
                            if k == 0:
                                pe.wait_ge(xn_done, b * TB + (t + 1))
                            last = pe.transpose(tp[k][:, P * t:P * (t + 1)], xn[:, t, P * k:P * (k + 1)],
                                                ident[:, :])
                        last.then_inc(tp_done, 1)

                def down(b, f, first):
                    pe.wait_ge(hhi_done, b * FT + (f + 1))
                    pe.wait_ge(hlo_done, b * FT + (f + 1))
                    if f == 0:
                        if first:
                            pe.wait_ge(weight_done, 9)
                        else:
                            pe.wait_ge(res_done, b * TB)
                    if first:
                        pe.wait_ge(whi_done, down_units(f))
                        pe.wait_ge(wlo_done, down_units(f))
                    r = rows(f)
                    for t in range(TB):
                        s = slice(P * t, P * (t + 1))
                        last_mm = products(pe, dp[t][:, :], h_hi[0:r, f % 2, s], h_lo[0:r, f % 2, s],
                                           wd_hi[0:r, f, :], wd_lo[0:r, f, :],
                                           start=(f == 0), stop=(f == FT - 1))
                    last_mm.then_inc(dp_done, 1)

                def body(b, first, last):
                    for f in range(FT):
                        r = rows(f)
                        bank = 0 if first else f % 2
                        if f == 0:
                            pe.wait_ge(hi_done, b * KH + KH)
                            pe.wait_ge(lo_done, b * KH + KH)
                        elif first:
                            pe.wait_ge(sg_done, f)
                            pe.wait_ge(hf_done, f)
                        elif f >= 2:
                            pe.wait_ge(sg_done, b * FT + (f - 1))
                            pe.wait_ge(hf_done, b * FT + (f - 1))
                        if first and f % 2 == 0 and f > 0:
                            pe.wait_ge(whi_done, pair_units(f // 2))
                            pe.wait_ge(wlo_done, pair_units(f // 2))
                        for i, (dst, c0, done) in enumerate(zip((gp[bank], up[bank]), columns(f),
                                                                (gate_done, up_done))):
                            s = slice(c0, c0 + r)
                            for k in range(KH):
                                if first and f == 0 and i == 0:
                                    pe.wait_ge(whi_done, k + 1)
                                    pe.wait_ge(wlo_done, k + 1)
                                last_mm = products(pe, dst[0:r, :], wg_hi[:, k, s], wg_lo[:, k, s],
                                                   xt_hi[:, k, :], xt_lo[:, k, :], start=(k == 0),
                                                   stop=(k == KH - 1))
                            last_mm.then_inc(done, 1)
                            if first:
                                for j in after(f, i):
                                    pick(j)
                        if f == FT - 1 and not last:
                            if first:
                                pe.wait_ge(weight_done, len(units))
                            else:
                                pe.wait_ge(sg_done, b * FT + (FT - 1))
                                pe.wait_ge(hf_done, b * FT + (FT - 1))
                            transposes(b + 1, range(0, 2))
                        if f >= 1:
                            down(b, f - 1, first)
                        if first:
                            for j in after(f, 2):
                                pick(j)
                    if not last:
                        pe.wait_ge(sg_done, b * FT + FT)
                        pe.wait_ge(hf_done, b * FT + FT)
                        transposes(b + 1, range(2, KH))
                    down(b, FT - 1, first)

                for i in BEFORE[:2]:
                    pick(i)
                transposes(0, range(KH))
                for i in BEFORE[2:]:
                    pick(i)
                batches(body)(pe)

            @block.scalar
            def _(act):
                def std_of(b):
                    act.wait_ge(ve_done, b + 1)
                    act.activation(std[:, :], var_e[:, :], ACT.Sqrt).then_inc(std_done, 1)

                def split_x(b, ks):
                    for k in ks:
                        act.wait_ge(tp_done, b * KH + (k + 1))
                        act.activation(xt_hi[:, k, :], tp[k][:, :], ACT.Copy).then_inc(hi_done, 1)

                def split_w(i):
                    _, _, _, kk, nn = units[i]
                    act.wait_ge(weight_done, i + 1)
                    act.activation(weights(wg_hi, wd_hi, i), q[0:kk, i % RQ, 0:nn].bitcast(F32),
                                   ACT.Copy).then_inc(whi_done, 1)

                def body(b, first, last):
                    for f in range(FT):
                        r = rows(f)
                        bank = 0 if first else f % 2
                        act.wait_ge(gate_done, b * FT + (f + 1))
                        if f >= 1 or not first:
                            act.wait_ge(hf_done, b * FT + f)
                        act.activation(sg[0:r, :], gp[bank][0:r, :], ACT.Silu).then_inc(sg_done, 1)
                        if first:
                            for i in after(f, 0):
                                split_w(i)
                        act.wait_ge(hf_done, b * FT + (f + 1))
                        if f >= 2 or not first:
                            act.wait_ge(dp_done, b * FT + (f - 1))
                        act.activation(h_hi[0:r, f % 2, :], hf[0:r, :], ACT.Copy).then_inc(hhi_done, 1)
                        if first:
                            for i in (*after(f, 1), *after(f, 2)):
                                split_w(i)
                        if f == 5 and not last:
                            std_of(b + 1)
                    if not last:
                        act.wait_ge(up_done, b * FT + FT)
                        split_x(b + 1, range(KH))

                std_of(0)
                for i in BEFORE[:2]:
                    split_w(i)
                split_x(0, range(KH))
                for i in BEFORE[2:]:
                    split_w(i)
                batches(body)(act)

            @block.gpsimd
            def _(pool):
                def rest_w(i):
                    _, _, _, kk, nn = units[i]
                    pool.wait_ge(whi_done, i + 1)
                    pool.tensor_tensor(weights(wg_lo, wd_lo, i), q[0:kk, i % RQ, 0:nn].bitcast(F32),
                                       weights(wg_hi, wd_hi, i).bitcast(F32), ALU.subtract).then_inc(wlo_done, 1)

                def body(b, first, last):
                    for f in range(FT):
                        r = rows(f)
                        if first:
                            for i in after(f, 0):
                                rest_w(i)
                        pool.wait_ge(hhi_done, b * FT + (f + 1))
                        if f >= 2 or not first:
                            pool.wait_ge(dp_done, b * FT + (f - 1))
                        pool.tensor_tensor(h_lo[0:r, f % 2, :], hf[0:r, :], h_hi[0:r, f % 2, :].bitcast(F32),
                                           ALU.subtract).then_inc(hlo_done, 1)
                        if first:
                            for i in (*after(f, 1), *after(f, 2)):
                                rest_w(i)

                pool.iota(pid[:, :], pattern=[[0, 1]], base=0, channel_multiplier=1).then_inc(pid_done, 1)
                for i in BEFORE:
                    rest_w(i)
                batches(body)(pool)

            @block.vector
            def _(dve):
                def norm_stats(b):
                    dve.wait_ge(x_in, b * 16 + 16)
                    for t in range(TB):
                        dve.bn_stats(stats[:, t, :], xn[:, t, :]).then_inc(st_done, 1)

                def norm_mean(b):
                    for t in range(TB):
                        dve.bn_aggr(mv[:, t, :], stats[:, t, :]).then_inc(mv_done, 1)

                def norm_var(b):
                    dve.wait_ge(mv_done, b * TB + TB)
                    dve.tensor_scalar(var_e[:, :], mv[:, :, 1], LN_EPS, None, ALU.add).then_inc(ve_done, 1)

                def norm_apply(b):
                    dve.wait_ge(std_done, b + 1)
                    dve.reciprocal(rstd[:, :], std[:, :]).then_inc(rstd_done, 1)
                    dve.wait_ge(rstd_done, b + 1)
                    for t in range(TB):
                        dve.tensor_scalar(xn[:, t, :], xn[:, t, :], mv[:, t, 0:1], rstd[:, t:t + 1],
                                          ALU.subtract, ALU.mult).then_inc(xn_done, 1)

                def rest_x(b):
                    for k in range(KH):
                        dve.wait_ge(hi_done, b * KH + (k + 1))
                        dve.tensor_tensor(xt_lo[:, k, :], tp[k][:, :], xt_hi[:, k, :].bitcast(F32),
                                          ALU.subtract).then_inc(lo_done, 1)

                def nibbles(i):
                    _, _, _, kk, nn = units[i]
                    dve.wait_ge(q_in[i % RQ], 16 * (i // RQ + 1))
                    n = q[0:kk, i % RQ, 0:nn]
                    dve.tensor_scalar(n, n, shift[0:kk, 0:1], 15, ALU.logical_shift_right,
                                      ALU.bitwise_and).then_inc(nib_done, 1)

                def weight(i):
                    _, _, _, kk, nn = units[i]
                    z, s = zero_scale_banks(i)
                    w = q[0:kk, i % RQ, 0:nn].bitcast(F32)
                    dve.wait_ge(nib_done, i + 1)
                    dve.wait_ge(picked, i + 1)
                    dve.tensor_tensor(w, q[0:kk, i % RQ, 0:nn], z[0:kk, 0:nn], ALU.subtract).then_inc(sub_done, 1)
                    dve.wait_ge(sub_done, i + 1)
                    dve.tensor_tensor(w, w, s[0:kk, 0:nn], ALU.mult).then_inc(weight_done, 1)
                    if i + 1 < len(units):
                        nibbles(i + 1)

                def body(b, first, last):
                    for f in range(FT):
                        r = rows(f)
                        bank = 0 if first else f % 2
                        if first:
                            for i in after(f, 0):
                                weight(i)
                        if f == 4 and not last:
                            dve.wait_ge(st_done, (b + 1) * TB + TB)
                        dve.wait_ge(sg_done, b * FT + (f + 1))
                        dve.wait_ge(up_done, b * FT + (f + 1))
                        if f >= 1 or not first:
                            dve.wait_ge(hhi_done, b * FT + f)
                            dve.wait_ge(hlo_done, b * FT + f)
                        dve.tensor_tensor(hf[0:r, :], sg[0:r, :], up[bank][0:r, :],
                                          ALU.mult).then_inc(hf_done, 1)
                        if first:
                            for i in (*after(f, 1), *after(f, 2)):
                                weight(i)
                        if not last:
                            if f == 3:
                                norm_stats(b + 1)
                            if f == 4:
                                norm_mean(b + 1)
                            if f == 5:
                                norm_var(b + 1)
                            if f == 7:
                                norm_apply(b + 1)
                    if not last:
                        rest_x(b + 1)
                    dve.wait_ge(dp_done, b * FT + FT)
                    dve.wait_ge(xr_in, b * 16 + 16)
                    for t in range(TB):
                        dve.tensor_tensor(xr[:, t, :], dp[t][:, :], xr[:, t, :], ALU.add).then_inc(res_done, 1)

                dve.wait_ge(pid_done, 1)
                dve.tensor_scalar(shift[:, :], pid[:, :], QC - 1, 2, ALU.bitwise_and,
                                  ALU.logical_shift_left).then_inc(shift_done, 1)
                dve.wait_ge(shift_done, 1)
                norm_stats(0)
                dve.wait_ge(st_done, TB)
                norm_mean(0)
                norm_var(0)
                nibbles(0)
                weight(0)
                norm_apply(0)
                weight(1)
                rest_x(0)
                for i in BEFORE[2:]:
                    weight(i)
                batches(body)(dve)


def kernel(**inputs):
    import numpy as np
    import concourse.bacc as bacc
    from concourse.bass_utils import run_bass_kernel_spmd as run

    get = lambda n: np.asarray(inputs[n])
    group_mean = np.zeros((SF, P), np.float32)
    for f0, f1 in ((0, R), (R, R + NS), (R + NS, SF)):
        group_mean[f0:f1, f0:f1] = 1.0 / (f1 - f0)
    cols = np.concatenate([np.arange(half + 2 * P * p, half + min(2 * P * (p + 1), INTER))
                           for p in range(PAIRS) for half in (0, INTER)])
    lay = {
        "x": get("L0_attn_hidden_states").reshape(NB, TB, P, H).transpose(0, 2, 1, 3),
        "w_in": get("L0_attn_W_in").reshape(2, DT, P, KH, P).transpose(4, 1, 0, 3, 2).reshape(P, DT, 2 * KH * P),
        "conv_w": get("L0_attn_conv_w").reshape(DT, P, TAPS).transpose(1, 0, 2),
        "conv_b": get("L0_attn_conv_b").reshape(DT, P).T,
        "w_x": get("L0_attn_W_x").T.reshape(DT, P, SF).transpose(1, 0, 2),
        "w_dt": np.concatenate([get("L0_attn_W_dt").T, get("L0_attn_b_dt")[None]], 0),
        "a_log": get("L0_attn_A_log").reshape(DT, P, NS).transpose(1, 0, 2),
        "d_skip": get("L0_attn_D").reshape(DT, P).T,
        "group_mean": group_mean,
        "w_out": get("L0_attn_W_out").T.reshape(DT, P, H).transpose(1, 0, 2),
        "qw_gu": get("L0_ffn_qweight_gu")[:, cols],
        "qw_d": get("L0_ffn_qweight_down"),
        "zeros": np.concatenate([get("L0_ffn_qzeros_gu")[:, cols[::QC] // QC].reshape(-1, P // QC),
                                 get("L0_ffn_qzeros_down").reshape(-1, P // QC)], 0),
        "scales": np.concatenate([get("L0_ffn_scales_gu")[:, cols].reshape(-1, P),
                                  get("L0_ffn_scales_down").reshape(-1, P)], 0),
        "g_idx": np.concatenate([get("L0_ffn_g_idx_gu"), get("L0_ffn_g_idx_down")])[None],
    }
    nc = bacc.Bacc("TRN2", target_bir_lowering=False, num_devices=1)
    arrays, args = {}, []
    for name, a in lay.items():
        a = np.ascontiguousarray(a)
        arrays[name] = a
        args.append(nc.dram_tensor(name, a.shape, mybir.dt.from_np(a.dtype), kind="ExternalInput").ap())
    args.append(nc.dram_tensor("out", (NB, P, TB, H), F32, kind="ExternalOutput").ap())
    build(nc, *args)
    r = run(nc, [arrays], core_ids=[0])
    return r.results[0]["out"].transpose(0, 2, 1, 3).reshape(NB, L, H)
```

```python
from contextlib import ExitStack
from itertools import compress

import concourse.bass as bass
from concourse import mybir

F32 = mybir.dt.float32
F32R = mybir.dt.float32r
U32 = mybir.dt.uint32
I32 = mybir.dt.int32
ALU = mybir.AluOpType
ACT = mybir.ActivationFunctionType

P = 128
NB, L, H = 4, 512, 512
DI, NS, R = 1024, 16, 32
TB = L // P
KH = H // P
DT = DI // P
SF = R + 2 * NS
TAPS = 4
INTER = 1376
FT = -(-INTER // P)
FL = INTER - (FT - 1) * P
GRP = 128
NG, NGD = H // GRP, INTER // GRP
LN_EPS, RMS_EPS = 1e-5, 1e-6
QC = 8
PAIRS = -(-FT // 2)
PC = 4 * P
QROWS = (NG * 2 * INTER + NGD * H) // P


def rows(ft):
    return P if ft < FT - 1 else FL


def products(pe, out, hi_l, lo_l, hi_r, lo_r, start, stop, **kw):
    pe.matmul(out, hi_l, hi_r, start=start, stop=False, **kw)
    pe.matmul(out, hi_l, lo_r, start=False, stop=False, **kw)
    return pe.matmul(out, lo_l, hi_r, start=False, stop=stop, **kw)


class Norm:
    def __init__(self, buffers, sem, stage):
        self.x, self.stats, self.mv, self.var_e, self.std, self.rstd = buffers
        self.x_in = [sem(f"{stage}_x_in{t}") for t in range(TB)]
        self.st_done, self.mv_done = sem(f"{stage}_st"), sem(f"{stage}_mv")
        self.ve_done, self.std_done = sem(f"{stage}_ve"), sem(f"{stage}_std")
        self.rstd_done, self.xn_done = sem(f"{stage}_rstd"), sem(f"{stage}_xn")


def norm_load(sp, n, src, b):
    for t in range(TB):
        sp.dma_start(n.x[:, t, :], src[bass.ds(b, 1), :, t].rearrange("o p h -> (o p) h")).then_inc(n.x_in[t], 16)


def norm_stats(dve, n, b):
    for t in range(TB):
        dve.wait_ge(n.x_in[t], b * 16 + 16)
        dve.bn_stats(n.stats[:, t, :], n.x[:, t, :]).then_inc(n.st_done, 1)


def norm_mean(dve, n, b):
    for t in range(TB):
        dve.bn_aggr(n.mv[:, t, :], n.stats[:, t, :]).then_inc(n.mv_done, 1)


def norm_var(dve, n, b):
    dve.wait_ge(n.mv_done, b * TB + TB)
    dve.tensor_scalar(n.var_e[:, :], n.mv[:, :, 1], LN_EPS, None, ALU.add).then_inc(n.ve_done, 1)


def norm_std(act, n, b):
    act.wait_ge(n.ve_done, b + 1)
    act.activation(n.std[:, :], n.var_e[:, :], ACT.Sqrt).then_inc(n.std_done, 1)


def norm_apply(dve, n, b):
    dve.wait_ge(n.std_done, b + 1)
    dve.reciprocal(n.rstd[:, :], n.std[:, :]).then_inc(n.rstd_done, 1)
    dve.wait_ge(n.rstd_done, b + 1)
    for t in range(TB):
        dve.tensor_scalar(n.x[:, t, :], n.x[:, t, :], n.mv[:, t, 0:1], n.rstd[:, t:t + 1],
                          ALU.subtract, ALU.mult).then_inc(n.xn_done, 1)


class Features:
    def __init__(self, sb, sem):
        self.gmean = sb("gmean", [SF, P])
        self.eps = sb("eps", [SF, 1])
        self.raw, self.square, self.rms, self.rinv, self.normed = (
            sb(f"feat_{n}", [SF, L]) for n in ("raw", "square", "rms", "rinv", "normed"))
        self.ts = sb("ts_split", [R, 2, L], F32R)
        self.raw_done, self.sq_done = sem("feat_done"), sem("sq_done")
        self.ms_done, self.rms_done = sem("ms_done"), sem("rms_done")
        self.rinv_done, self.fn_done = sem("rinv_done"), sem("fn_done")
        self.tshi_done, self.tslo_done = sem("tshi_done"), sem("tslo_done")
        self.out = sem("feat_out")




def mean_squares(pe, ft, bank, b):
    pe.wait_ge(ft.sq_done, b)
    pe.matmul(bank[:, :], ft.gmean[:, :], ft.square[:, :], start=True, stop=True).then_inc(ft.ms_done, 1)


def root_mean_squares(act, ft, bank, b):
    act.wait_ge(ft.ms_done, b)
    act.activation(ft.rms[:, :], bank[0:SF, :], ACT.Sqrt, bias=ft.eps[:, 0:1]).then_inc(ft.rms_done, 1)


def norm_features(dve, ft, b):
    dve.wait_ge(ft.rms_done, b)
    dve.reciprocal(ft.rinv[:, :], ft.rms[:, :]).then_inc(ft.rinv_done, 1)
    dve.wait_ge(ft.rinv_done, b)
    dve.wait_ge(ft.out, (b - 1) * 32 + 1)
    dve.tensor_tensor(ft.normed[:, :], ft.raw[:, :], ft.rinv[:, :], ALU.mult).then_inc(ft.fn_done, 1)


def split_ts(act, ft, b):
    act.wait_ge(ft.fn_done, b)
    act.activation(ft.ts[:, 0, :], ft.normed[0:R, :], ACT.Copy).then_inc(ft.tshi_done, 1)


def rest_ts(dve, ft, b):
    dve.wait_ge(ft.tshi_done, b)
    dve.tensor_tensor(ft.ts[:, 1, :], ft.normed[0:R, :], ft.ts[:, 0, :].bitcast(F32),
                      ALU.subtract).then_inc(ft.tslo_done, 1)


def store_features(sp, ft, bc_d, ts_d, b):
    sp.wait_ge(ft.fn_done, b)
    sp.dma_start(bc_d[bass.ds(b - 1, 1)].rearrange("o n l -> (o n) l"), ft.normed[R:SF, :]).then_inc(ft.out, 16)
    sp.wait_ge(ft.tslo_done, b)
    sp.dma_start(ts_d[bass.ds(b - 1, 1)].rearrange("o r s l -> (o r) s l"),
                 ft.ts[:, :, :].bitcast(F32)).then_inc(ft.out, 16)


def build(nc, x, w_in, conv_w, conv_b, w_x, w_dt, a_log, d_skip, group_mean, w_out,
          qw_gu, qw_d, zeros, scales, g_idx, out):
    u_d = nc.dram_tensor("u_scratch", (NB, DT, P, L), F32, kind="Internal").ap()
    g_d = nc.dram_tensor("gate_scratch", (NB, DT, P, L), F32, kind="Internal").ap()
    bc_d = nc.dram_tensor("bc_scratch", (NB, 2 * NS, L), F32, kind="Internal").ap()
    x1_d = nc.dram_tensor("x1_scratch", (NB, P, TB, H), F32, kind="Internal").ap()
    ts_d = nc.dram_tensor("ts_scratch", (NB, R, 2, L), F32, kind="Internal").ap()

    hot_d = nc.dram_tensor("hot_scratch", (NGD, H + INTER), F32, kind="Internal").ap()
    rows_d = nc.dram_tensor("rows_scratch", (3, QROWS * P), F32, kind="Internal").ap()

    whole = ExitStack()
    with whole:
        def tensors(ctx):
            def sb(name, shape, dt=F32):
                return ctx.enter_context(nc.sbuf_tensor(name, shape, dt))

            def ps(name, shape):
                return ctx.enter_context(nc.psum_tensor(name, shape, F32))

            def sem(name):
                return ctx.enter_context(nc.semaphore(name))
            return sb, ps, sem

        sb, ps, sem = tensors(whole)
        ident = sb("ident", [P, P])
        a_neg = sb("a_neg", [P, DT, NS])
        dsk = sb("dsk", [P, DT])
        norm_buffers = (sb("xn", [P, TB, H]), sb("stats", [P, TB, 6]), sb("mv", [P, TB, 2]),
                        sb("var_e", [P, TB]), sb("std", [P, TB]), sb("rstd", [P, TB]))
        stream = sb("stream", [P, TB, H])
        x1_out = sem("x1_out")
        ffn_norm = Norm(norm_buffers, sem, "ffn")
        with ExitStack() as c:
            sbo, _, semo = tensors(c)
            wdt_hi, wdt_lo = sbo("wdt_hi", [R + 1, DI], F32R), sbo("wdt_lo", [R + 1, DI], F32R)
            ts_hl = sbo("ts_hl", [R + 1, 2, L], F32R)
            ts_in = semo("ts_in")
            ft = Features(sbo, semo)
            project(nc, tensors, Norm(norm_buffers, semo, "project"), ft, stream, ts_in, wdt_hi, wdt_lo,
                    ts_hl, ident, a_neg, dsk, x, w_in, conv_w, conv_b, w_x, w_dt, a_log, d_skip, group_mean,
                    zeros, scales, g_idx, u_d, g_d, bc_d, ts_d, hot_d, rows_d)
            scan(nc, tensors, ffn_norm, ft, ts_in, stream, x1_out, ident, a_neg, dsk, wdt_hi, wdt_lo, ts_hl,
                 x, w_out, u_d, g_d, bc_d, ts_d, x1_d)
        ffn(nc, tensors, ffn_norm, stream, x1_out, x1_d, hot_d, rows_d, ident, qw_gu, qw_d, out)


def project(nc, tensors, norm, ft, stream, ts_in, wdt_hi, wdt_lo, ts_hl, ident, a_neg, dsk, x, w_in,
            conv_w, conv_b, w_x, w_dt, a_log, d_skip, group_mean, zeros, scales, g_idx, u_d, g_d, bc_d, ts_d,
            hot_d, rows_d):
    NR = 3
    with ExitStack() as c:
        sb, ps, sem = tensors(c)
        wraw = sb("wraw", [P, DT, 2 * KH * P])
        win_hi, win_lo = sb("win_hi", [P, DT, 2 * KH * P], F32R), sb("win_lo", [P, DT, 2 * KH * P], F32R)
        wxraw = sb("wxraw", [P, DT, SF])
        wx_hi, wx_lo = sb("wx_hi", [P, DT, SF], F32R), sb("wx_lo", [P, DT, SF], F32R)
        wdraw = sb("wdraw", [R + 1, DI])
        cw, cb = sb("cw", [P, DT, TAPS]), sb("cb", [P, DT])
        xn = norm.x
        xt_hi, xt_lo = sb("xt_hi", [P, KH, L], F32R), sb("xt_lo", [P, KH, L], F32R)
        xc = sb("xc", [P, 2, L])
        u, g = stream[:, 0:2, :], stream[:, 2:4, :]
        u_hi, u_lo = sb("u_hi", [P, 2, L], F32R), sb("u_lo", [P, 2, L], F32R)
        gi = sb("gi", [NGD, H + INTER], I32)
        hot = sb("hot", [NGD, H + INTER])
        hot_r = sb("hot_r", [NGD, H + INTER], F32R)
        pid, pidf = sb("pid", [P, 1], U32), sb("pidf", [P, 1])
        zw, zn = sb("zero_words", [QROWS, P // QC], U32), sb("zero_nibbles", [QROWS, P], U32)
        zr = sb("zero_rows", [QROWS, P], F32R)
        sf = sb("scale_rows", [QROWS, P])
        s_hi, s_lo = sb("scale_hi", [QROWS, P], F32R), sb("scale_lo", [QROWS, P], F32R)
        tp = [ps(f"tp{i}", [P, L]) for i in range(KH)]
        ip = [ps(f"ip{i}", [P, L]) for i in range(NR)]
        fp = ps("fp", [SF, L])
        ms = tp[KH - 1]

        w_in_s = [sem(f"w_in{m}") for m in range(DT)]
        small_in = sem("small_in")
        w_split, w_rest = sem("w_split"), sem("w_rest")
        wx_split, wx_rest = sem("wx_split"), sem("wx_rest")
        ones_done, eps_done = sem("ones_done"), sem("eps_done")
        id_zero, id_done = sem("id_zero"), sem("id_done")
        tp_done = sem("tp_done")
        hi_done, lo_done = sem("hi_done"), sem("lo_done")
        ip_done = sem("ip_done")
        xc_first = sem("xc_first")
        tap_step, taps_done = sem("tap_step"), sem("taps_done")
        u_done, uhi_done, ulo_done = sem("u_done"), sem("uhi_done"), sem("ulo_done")
        g_done = sem("g_done")
        wx_used = sem("wx_used")
        u_out = [sem(f"u_out{i}") for i in range(2)]
        g_out = [sem(f"g_out{i}") for i in range(2)]
        quant_in, pid_done, pidf_done = sem("quant_in"), sem("pid_done"), sem("pidf_done")
        hot_step, hot_done = sem("hot_step"), sem("hot_done")
        nibble_done, zero_done = sem("nibble_done"), sem("zero_done")
        scale_hi_done, scale_lo_done, quant_out = sem("scale_hi_done"), sem("scale_lo_done"), sem("quant_out")

        def batches(body):
            def run(eng):
                body(0, True, False)
                with eng.Fori(1, NB - 1) as b:
                    body(b, False, False)
                body(NB - 1, False, True)
            return run

        with nc.Block() as block:
            @block.sync
            def _(sp):
                norm_load(sp, norm, x, 0)
                sp.dma_start(wraw[:, 0, :], w_in[:, 0, :]).then_inc(w_in_s[0], 16)
                for dst, src in ((wxraw[:, :, :], w_x), (wdraw[:, :], w_dt), (a_neg[:, :, :], a_log),
                                 (dsk[:, :], d_skip), (cw[:, :, :], conv_w), (cb[:, :], conv_b),
                                 (ft.gmean[:, :], group_mean)):
                    sp.dma_start(dst, src).then_inc(small_in, 16)
                for m in range(1, DT):
                    sp.dma_start(wraw[:, m, :], w_in[:, m, :]).then_inc(w_in_s[m], 16)

                def body(b, first, last):
                    if not last:
                        sp.wait_ge(tp_done, b * KH + KH)
                        norm_load(sp, norm, x, b + 1)
                    for m in range(DT):
                        for done, dst, src, out in ((u_done, u_d, u, u_out), (g_done, g_d, g, g_out)):
                            sp.wait_ge(done, b * DT + (m + 1))
                            sp.dma_start(dst[bass.ds(b, 1), m].rearrange("o p l -> (o p) l"),
                                         src[:, m % 2, :]).then_inc(out[m % 2], 16)
                        if m == 5 and not first:
                            store_features(sp, ft, bc_d, ts_d, b)

                for dst, src in ((zw, zeros), (sf, scales), (gi, g_idx.broadcast_to([NGD, H + INTER]))):
                    sp.dma_start(dst[:, :], src).then_inc(quant_in, 16)
                batches(body)(sp)
                sp.wait_ge(ft.out, 1 + 32)
                sp.dma_start(ts_hl[0:R, :, :].bitcast(F32), ts_d[0]).then_inc(ts_in, 16)
                for done, n, dst, src in ((zero_done, 1, rows_d[0], zr), (scale_hi_done, 1, rows_d[1], s_hi),
                                          (scale_lo_done, 1, rows_d[2], s_lo)):
                    sp.wait_ge(done, n)
                    sp.dma_start(dst.rearrange("(p c) -> p c", c=P),
                                 src[:, :].bitcast(F32)).then_inc(quant_out, 16)
                sp.wait_ge(hot_done, 1)
                sp.dma_start(hot_d, hot_r[:, :].bitcast(F32)).then_inc(quant_out, 16)
                sp.wait_ge(quant_out, 16 * 4)
                for done in (*u_out, *g_out):
                    sp.wait_ge(done, 16 * NB * DT // 2)

            @block.tensor
            def _(pe):
                def transposes(b):
                    for k in range(KH):
                        for t in range(TB):
                            if k == 0:
                                pe.wait_ge(norm.xn_done, b * TB + (t + 1))
                            last = pe.transpose(tp[k][:, P * t:P * (t + 1)], xn[:, t, P * k:P * (k + 1)],
                                                ident[:, :])
                        last.then_inc(tp_done, 1)

                def features(b, m):
                    pe.wait_ge(uhi_done, b * DT + (m + 1))
                    pe.wait_ge(ulo_done, b * DT + (m + 1))
                    products(pe, fp[:, :], wx_hi[:, m, :], wx_lo[:, m, :], u_hi[:, m % 2, :], u_lo[:, m % 2, :],
                             start=(m == 0), stop=(m == DT - 1)).then_inc(wx_used, 1)

                def body(b, first, last):
                    for j in range(2 * DT):
                        m, gate = j // 2, j % 2
                        if first and not gate:
                            pe.wait_ge(w_rest, m + 1)
                        if j >= NR or not first:
                            jj = j - NR if j >= NR else (2 * DT - 1, 2 * DT - 3, 2 * DT - 2)[j] - 2 * DT
                            pe.wait_ge(g_done if jj % 2 else taps_done, b * DT + (jj // 2 + 1))
                        for k in range(KH):
                            if j == 0:
                                pe.wait_ge(hi_done, b * KH + (k + 1))
                                pe.wait_ge(lo_done, b * KH + (k + 1))
                            s = slice((gate * KH + k) * P, (gate * KH + k + 1) * P)
                            last_mm = products(pe, ip[j % NR][:, :], win_hi[:, m, s], win_lo[:, m, s],
                                               xt_hi[:, k, :], xt_lo[:, k, :], start=(k == 0),
                                               stop=(k == KH - 1))
                        last_mm.then_inc(ip_done, 1)
                        if j == 2 and not first:
                            mean_squares(pe, ft, ms, b)
                        if gate and m >= 1:
                            if m == 1 and first:
                                pe.wait_ge(wx_rest, 2)
                            if m == 1 and not first:
                                pe.wait_ge(ft.raw_done, b)
                            features(b, m - 1)
                    if not last:
                        if not first:
                            pe.wait_ge(ft.rms_done, b)
                        transposes(b + 1)
                    features(b, DT - 1)

                pe.wait_ge(id_done, 1)
                transposes(0)
                batches(body)(pe)
                mean_squares(pe, ft, ms, NB)

            @block.scalar
            def _(act):
                def split_w(m):
                    act.wait_ge(w_in_s[m], 16)
                    act.activation(win_hi[:, m, :], wraw[:, m, :], ACT.Copy).then_inc(w_split, 1)

                def split_x(b):
                    for k in range(KH):
                        act.wait_ge(tp_done, b * KH + (k + 1))
                        if k == 0 and not (isinstance(b, int) and b == 0):
                            act.wait_ge(ip_done, b * 2 * DT)
                        act.activation(xt_hi[:, k, :], tp[k][:, :], ACT.Copy).then_inc(hi_done, 1)

                def body(b, first, last):
                    for m in range(DT):
                        if first and m + 2 < DT:
                            split_w(m + 2)
                        act.wait_ge(ip_done, b * 2 * DT + (2 * m + 1))
                        if m >= 2 or not first:
                            act.wait_ge(u_done, b * DT + (m - 1))
                        act.activation(xc[:, m % 2, :], ip[(2 * m) % NR][:, :], ACT.Identity,
                                       bias=cb[:, m:m + 1], scale=cw[:, m, TAPS - 1:TAPS]).then_inc(xc_first, 1)
                        act.wait_ge(ip_done, b * 2 * DT + (2 * m + 2))
                        if m >= 2 or not first:
                            act.wait_ge(g_out[m % 2], b * (8 * DT) + 16 * (m // 2))
                        act.activation(g[:, m % 2, :], ip[(2 * m + 1) % NR][:, :], ACT.Silu).then_inc(g_done, 1)
                        act.wait_ge(taps_done, b * DT + (m + 1))
                        if m >= 2 or not first:
                            act.wait_ge(u_out[m % 2], b * (8 * DT) + 16 * (m // 2))
                            act.wait_ge(ulo_done, b * DT + (m - 1))
                            act.wait_ge(wx_used, b * DT + (m - 1))
                        act.activation(u[:, m % 2, :], xc[:, m % 2, :], ACT.Silu).then_inc(u_done, 1)
                        act.wait_ge(u_done, b * DT + (m + 1))
                        act.activation(u_hi[:, m % 2, :], u[:, m % 2, :], ACT.Copy).then_inc(uhi_done, 1)
                        if m == 1 and not first:
                            root_mean_squares(act, ft, ms, b)
                        if m == 4 and not first:
                            split_ts(act, ft, b)
                        if m == 4 and not last:
                            norm_std(act, norm, b + 1)
                    if not last:
                        split_x(b + 1)
                    act.wait_ge(wx_used, b * DT + DT)
                    act.activation(ft.raw[:, :], fp[:, :], ACT.Copy).then_inc(ft.raw_done, 1)
                    act.wait_ge(ft.raw_done, b + 1)
                    act.activation(ft.square[:, :], ft.raw[:, :], ACT.Square).then_inc(ft.sq_done, 1)

                norm_std(act, norm, 0)
                split_w(0)
                split_x(0)
                split_w(1)
                act.wait_ge(small_in, 16 * 7)
                act.activation(wx_hi[:, :, :], wxraw[:, :, :], ACT.Copy).then_inc(wx_split, 1)
                act.activation(wdt_hi[:, :], wdraw[:, :], ACT.Copy).then_inc(wx_split, 1)
                act.wait_ge(eps_done, 1)
                batches(body)(act)
                root_mean_squares(act, ft, ms, NB)

            @block.vector
            def _(dve):
                def rest_w(m):
                    dve.wait_ge(w_split, m + 1)
                    dve.tensor_tensor(win_lo[:, m, :], wraw[:, m, :], win_hi[:, m, :].bitcast(F32),
                                      ALU.subtract).then_inc(w_rest, 1)

                def rest_x(b):
                    for k in range(KH):
                        dve.wait_ge(hi_done, b * KH + (k + 1))
                        dve.tensor_tensor(xt_lo[:, k, :], tp[k][:, :], xt_hi[:, k, :].bitcast(F32),
                                          ALU.subtract).then_inc(lo_done, 1)

                def zero_rows():
                    dve.wait_ge(quant_in, 16 * 3)
                    for j in range(QC):
                        dve.tensor_scalar(zn[:, :].rearrange("g (c j) -> g c j", j=QC)[:, :, j], zw[:, :], 4 * j,
                                          15, ALU.logical_shift_right, ALU.bitwise_and).then_inc(nibble_done, 1)
                    dve.wait_ge(nibble_done, QC)
                    dve.tensor_scalar(zr[:, :], zn[:, :], 1.0, None, ALU.add).then_inc(zero_done, 1)

                def scale_rows():
                    dve.tensor_copy(s_hi[:, :], sf[:, :]).then_inc(scale_hi_done, 1)
                    dve.wait_ge(scale_hi_done, 1)
                    dve.tensor_tensor(s_lo[:, :], sf[:, :], s_hi[:, :].bitcast(F32),
                                      ALU.subtract).then_inc(scale_lo_done, 1)

                parts = ((slice(0, H), NG), (slice(H, H + INTER), NGD))

                def wrap_index():
                    wrap = gi[:, :].bitcast(F32)
                    dve.tensor_copy(hot[:, :], gi[:, :]).then_inc(hot_step, 1)
                    dve.wait_ge(hot_step, 1)
                    for s, n in parts:
                        dve.tensor_scalar(wrap[:, s], hot[:, s], 0.0, float(n), ALU.is_lt,
                                          ALU.mult).then_inc(hot_step, 1)
                    dve.wait_ge(hot_step, 3)
                    dve.tensor_tensor(hot[:, :], hot[:, :], wrap, ALU.add).then_inc(hot_step, 1)

                def clamp_index():
                    dve.wait_ge(hot_step, 4)
                    for s, n in parts:
                        dve.tensor_scalar(hot[:, s], hot[:, s], 0.0, float(n - 1), ALU.max,
                                          ALU.min).then_inc(hot_step, 1)

                def one_hot():
                    dve.wait_ge(hot_step, 6)
                    dve.wait_ge(pidf_done, 1)
                    dve.tensor_scalar(hot[:, :], hot[:, :], pidf[0:NGD, 0:1], None,
                                      ALU.is_equal).then_inc(hot_step, 1)
                    dve.wait_ge(hot_step, 7)
                    dve.tensor_copy(hot_r[:, :], hot[:, :]).then_inc(hot_done, 1)

                def body(b, first, last):
                    for m in range(DT):
                        if first and m + 2 < DT:
                            rest_w(m + 2)
                        if m == 2 and not last:
                            dve.wait_ge(norm.st_done, (b + 1) * TB + TB)
                        for j in range(TAPS - 1):
                            s = TAPS - 1 - j
                            if j == 0:
                                dve.wait_ge(xc_first, b * DT + (m + 1))
                            else:
                                dve.wait_ge(tap_step, b * DT * (TAPS - 2) + (m * (TAPS - 2) + j))
                            dve.scalar_tensor_tensor(
                                out=xc[:, m % 2, s:], in0=ip[(2 * m) % NR][:, 0:L - s],
                                scalar=cw[:, m, j:j + 1], in1=xc[:, m % 2, s:], op0=ALU.mult,
                                op1=ALU.add).then_inc(taps_done if j == TAPS - 2 else tap_step, 1)
                        if not last:
                            if m == 1:
                                norm_stats(dve, norm, b + 1)
                            if m == 2:
                                norm_mean(dve, norm, b + 1)
                            if m == 3:
                                norm_var(dve, norm, b + 1)
                            if m == 5:
                                norm_apply(dve, norm, b + 1)
                        if not first:
                            if m == 3:
                                norm_features(dve, ft, b)
                            if m == 4:
                                rest_ts(dve, ft, b)
                        if last:
                            if m == 0:
                                zero_rows()
                                scale_rows()
                            if m == 1:
                                wrap_index()
                            if m == 2:
                                clamp_index()
                            if m == 5:
                                one_hot()
                    if not last:
                        rest_x(b + 1)

                dve.memset(ft.eps[:, :], RMS_EPS).then_inc(eps_done, 1)
                dve.memset(ft.normed[0:1, 0:1], 0.0).then_inc(ft.out, 1)
                dve.wait_ge(pid_done, 1)
                dve.tensor_copy(pidf[:, :], pid[:, :]).then_inc(pidf_done, 1)
                dve.memset(ts_hl[R:R + 1, 0, :].bitcast(F32), 1.0).then_inc(ones_done, 1)
                dve.memset(ts_hl[R:R + 1, 1, :].bitcast(F32), 0.0).then_inc(ones_done, 1)
                norm_stats(dve, norm, 0)
                dve.wait_ge(norm.st_done, TB)
                norm_mean(dve, norm, 0)
                norm_var(dve, norm, 0)
                norm_apply(dve, norm, 0)
                rest_w(0)
                rest_x(0)
                rest_w(1)
                dve.wait_ge(wx_split, 2)
                dve.tensor_tensor(wx_lo[:, :, :], wxraw[:, :, :], wx_hi[:, :, :].bitcast(F32),
                                  ALU.subtract).then_inc(wx_rest, 1)
                dve.tensor_tensor(wdt_lo[:, :], wdraw[:, :], wdt_hi[:, :].bitcast(F32),
                                  ALU.subtract).then_inc(wx_rest, 1)
                batches(body)(dve)

            @block.gpsimd
            def _(pool):
                pool.iota(pid[:, :], pattern=[[0, 1]], base=0, channel_multiplier=1).then_inc(pid_done, 1)
                pool.memset(ident[:, :], 0.0).then_inc(id_zero, 1)
                pool.wait_ge(id_zero, 1)
                pool.affine_select(out=ident[:, :], in_=ident[:, :], compare_op=ALU.not_equal, fill=1.0,
                                   base=0, pattern=[[-1, P]], channel_multiplier=1).then_inc(id_done, 1)

                def body(b, first, last):
                    for m in range(DT):
                        pool.wait_ge(uhi_done, b * DT + (m + 1))
                        pool.tensor_tensor(u_lo[:, m % 2, :], u[:, m % 2, :],
                                           u_hi[:, m % 2, :].bitcast(F32), ALU.subtract).then_inc(ulo_done, 1)

                batches(body)(pool)


def scan(nc, tensors, norm, ft, ts_in, xr, x1_out, ident, a_neg, dsk, wdt_hi, wdt_lo, ts_hl,
         x, w_out, u_d, g_d, bc_d, ts_d, x1_d):
    RA, RW, NQ = 4, 8, 4
    NI = NS // 2
    OWN = 2
    AT_EXP, AT_LN, AT_SUM, AT_GAIN, AT_DT, AT_OUT = 2, 4, 5, 7, 6, 1
    UNITS = DT * NI
    NL = NS // NQ
    with ExitStack() as c:
        sb, ps, sem = tensors(c)
        wo = sb("wo", [P, DT, H])
        bb, cc = sb("bb", [P, NS, L]), sb("cc", [P, NS, L])
        u, g = sb("u_s", [P, 2, L]), sb("g_s", [P, 2, L])
        dt, dtu = sb("dt", [P, 2, L]), sb("dtu", [P, 2, L])
        sp1, sp2 = sb("sp1", [P, L]), sb("sp2", [P, L])
        decay = sb("decay", [P, RA, 2, L])
        work = sb("work", [P, RW, 2, L])
        yg = sb("yg", [P, 2, L])
        one = sb("one", [P, 1])
        d_diag = sb("d_diag", [P, DT, P])
        dtp = ps("dtp", [P, L])
        yp = [ps(f"yp{i}", [P, L]) for i in range(2)]
        op = [ps(f"op{t}", [P, H]) for t in range(TB)]

        wo_in, diag_done, one_done = sem("wo_in"), sem("diag_done"), sem("one_done")
        bb_in = [sem(f"bb_in{q}") for q in range(NQ)]
        cc_in = [sem(f"cc_in{q}") for q in range(NQ)]
        u_in = [sem(f"u_in{i}") for i in range(2)]
        g_in = [sem(f"g_in{i}") for i in range(2)]
        dtp_done = sem("dtp_done")
        abs_done, e_done, w_done, ln_done = sem("abs_done"), sem("e_done"), sem("w_done"), sem("ln_done")
        round_done, log_done = sem("round_done"), sem("log_done")
        dt_done, dtu_done = sem("dt_done"), sem("dtu_done")
        decay_done, drive_done = sem("decay_done"), sem("drive_done")
        h_done, prod_done = sem("h_done"), sem("prod_done")
        unit_summed = sem("unit_summed")
        y_done = sem("y_done")
        yg_done = sem("yg_done")
        a_exp, a_done = sem("a_exp"), sem("a_done")
        op_done, res_done = sem("op_done"), sem("res_done")
        block_done = sem("x1_block_done")
        own_done = sem("own_done")
        skip_done = sem("skip_done")

        x_in = sem("xr_in")
        reset_done = sem("reset_done")

        def batches(eng, body):
            body(0, True, False)
            with eng.Fori(1, NB - 1) as b:
                body(b, False, False)
            body(NB - 1, False, True)

        with nc.Block() as block:
            @block.sync
            def _(sp):
                def load_ts(b):
                    sp.dma_start(ts_hl[0:R, :, :].bitcast(F32), ts_d[bass.ds(b, 1)].rearrange(
                        "o r s l -> (o r) s l")).then_inc(ts_in, 16)

                def load_bc(b, q, only=(True, True)):
                    s = slice(q * NL, (q + 1) * NL)
                    for dst, off, done in compress(((bb, 0, bb_in), (cc, NS, cc_in)), only):
                        src = bc_d[bass.ds(b, 1), off + s.start:off + s.stop].rearrange(
                            "o n l -> o (n l)").broadcast_to([P, NL * L])
                        sp.dma_start(dst[:, s, :].rearrange("p n l -> p (n l)"), src).then_inc(done[q], 16)

                def load_ug(b, d, only=(True, True)):
                    for dst, src, done in compress(((u, u_d, u_in), (g, g_d, g_in)), only):
                        sp.dma_start(dst[:, d % 2, :], src[bass.ds(b, 1), d].rearrange(
                            "o p l -> (o p) l")).then_inc(done[d % 2], 16)

                def load_x(b):
                    sp.dma_start(xr[:, :, :], x[bass.ds(b, 1)].rearrange("o p t h -> (o p) t h")).then_inc(x_in, 16)

                def store_x1(b):
                    sp.wait_ge(res_done, b * TB)
                    sp.dma_start(x1_d[bass.ds(b - 1, 1)].rearrange("o p t h -> (o p) t h"),
                                 xr[:, :, :]).then_inc(x1_out, 16)

                load_ug(0, 0, (True, False))
                for q in range(NQ + 1):
                    if q < NQ:
                        load_bc(0, q, (True, False))
                    if q >= 1:
                        load_bc(0, q - 1, (False, True))
                    if q == NQ // 2:
                        load_ug(0, 1, (True, False))
                load_ug(0, 0, (False, True))
                load_ug(0, 1, (False, True))
                sp.dma_start(wo[:, :, :], w_out).then_inc(wo_in, 16)
                load_x(0)
                store_features(sp, ft, bc_d, ts_d, NB)
                sp.wait_ge(ft.out, 1 + 32 * NB)

                def body(b, first, last):
                    if last:
                        norm_load(sp, norm, x1_d, 0)
                    for d in range(1 if not first else 2, DT):
                        sp.wait_ge(yg_done, b * DT + (d - 1))
                        load_ug(b, d)
                        if d == 3 and not first:
                            store_x1(b)
                            sp.wait_ge(x1_out, b * 16)
                            load_x(b)
                    if last:
                        store_x1(NB)
                        return
                    sp.wait_ge(dtp_done, b * DT + DT)
                    load_ts(b + 1)
                    sp.wait_ge(yg_done, b * DT + (DT - 1))
                    load_ug(b + 1, 0)
                    for q in range(NQ):
                        sp.wait_ge(prod_done, b * UNITS + (UNITS - NI + (q + 1) * NI // NQ))
                        load_bc(b + 1, q)

                batches(sp, body)

            @block.tensor
            def _(pe):
                def dt_product(b, d):
                    if d == 0:
                        pe.wait_ge(ts_in, b * 16 + 16)
                    s = slice(P * d, P * (d + 1))
                    products(pe, dtp[:, :], wdt_hi[:, s], wdt_lo[:, s], ts_hl[:, 0, :],
                             ts_hl[:, 1, :], start=True, stop=True).then_inc(dtp_done, 1)

                def out_product(b, d):
                    pe.wait_ge(yg_done, b * DT + (d + 1))
                    for t in range(TB):
                        s = slice(P * t, P * (t + 1))
                        last = pe.matmul(op[t][:, :], yg[:, d % 2, s], wo[:, d % DT, :], start=(d == 0),
                                         stop=(d % DT == DT - 1))
                        if isinstance(b, int) and (b, d) == (NB - 1, DT - 1) and t < TB - 1:
                            last.then_inc(block_done, 1)
                    last.then_inc(op_done, 1)

                def body(b, first, last):
                    for d in range(DT):
                        for i in range(NI):
                            k = d * NI + i
                            pe.wait_ge(prod_done, b * UNITS + (k + 1))
                            if i == 0 and (d >= 2 or not first):
                                pe.wait_ge(yg_done, b * DT + (d - 1))
                            pe.matmul(yp[d % 2][:, :], ident[:, :], work[:, k % RW, 0, :],
                                      start=(i == 0), stop=False)
                            pe.matmul(yp[d % 2][:, :], ident[:, :], work[:, k % RW, 1, :],
                                      start=False, stop=False).then_inc(unit_summed, 1)
                            if i == AT_DT and not (last and d >= DT - 2):
                                pe.wait_ge(dt_done, b * DT + (d + 2))
                                dt_product(*((b, d + 2) if d + 2 < DT else (b + 1, d + 2 - DT)))
                            if i == AT_OUT and not (first and d == 0):
                                if d == 0:
                                    out_product(b, -1)
                                else:
                                    if d == 1 and first:
                                        pe.wait_ge(wo_in, 16)
                                    if d == 1 and not first:
                                        pe.wait_ge(res_done, b * TB)
                                    out_product(b, d - 1)
                            if d == 5 and i < TB:
                                if i == 0:
                                    pe.wait_ge(x_in, b * 16 + 16)
                                skip = pe.matmul(op[i][:, :], ident[:, :], xr[:, i, :], start=False, stop=False)
                                if i == TB - 1:
                                    skip.then_inc(skip_done, 1)
                        pe.wait_ge(u_in[d % 2], b * (8 * DT) + 16 * (d // 2 + 1))
                        if d == 0 and first:
                            pe.wait_ge(diag_done, DT)
                        pe.matmul(yp[d % 2][:, :], d_diag[:, d, :], u[:, d % 2, :], start=False,
                                  stop=True).then_inc(y_done, 1)
                    if last:
                        out_product(b, DT - 1)

                dt_product(0, 0)
                pe.wait_ge(dt_done, 1)
                dt_product(0, 1)
                batches(pe, body)

            @block.scalar
            def _(act):
                act.preload_act_table_set("natural_log_exp_and_others")
                act.activation(a_neg[:, :, :], a_neg[:, :, :], ACT.Exp).then_inc(a_exp, 1)
                act.wait_ge(a_exp, 1)
                act.activation(a_neg[:, :, :], a_neg[:, :, :], ACT.Copy, scale=-1.0).then_inc(a_done, 1)
                def softplus_exp(b, d):
                    act.wait_ge(dtp_done, b * DT + (d + 1))
                    act.activation(sp1[:, :], dtp[:, :], ACT.Abs).then_inc(abs_done, 1)
                    act.wait_ge(abs_done, b * DT + (d + 1))
                    act.activation(sp1[:, :], sp1[:, :], ACT.Exp, scale=-1.0).then_inc(e_done, 1)
                    act.wait_ge(e_done, b * DT + (d + 1))
                    act.activation(sp2[:, :], sp1[:, :], ACT.Identity, bias=one[:, 0:1]).then_inc(w_done, 1)

                def softplus_log(b, d):
                    act.wait_ge(round_done, b * DT + (d + 1))
                    act.activation(sp2[:, :], sp2[:, :], ACT.Ln).then_inc(ln_done, 1)

                def residual(b):
                    act.wait_ge(skip_done, b)
                    for t in range(TB):
                        if isinstance(b, int) and b == NB and t < TB - 1:
                            act.wait_ge(block_done, t + 1)
                        else:
                            act.wait_ge(op_done, b * DT)
                        act.activation(xr[:, t, :], op[t][:, :], ACT.Copy).then_inc(res_done, 1)

                def body(b, first, last):
                    for d in range(DT):
                        ahead = (b, d + 1) if d + 1 < DT else (b + 1, 0)
                        more = d + 1 < DT or not last
                        act.wait_ge(dt_done, b * DT + (d + 1))
                        for i in range(NI):
                            k = d * NI + i
                            if not first or k >= RA:
                                act.wait_ge(h_done, b * UNITS + (k - RA + 1))
                            for m in range(2):
                                n = 2 * i + m
                                done = act.activation(decay[:, k % RA, m, 1:], dt[:, d % 2, 1:], ACT.Exp,
                                                      scale=a_neg[:, d, n:n + 1])
                            done.then_inc(decay_done, 1)
                            if i == AT_EXP and more:
                                softplus_exp(*ahead)
                            if i == AT_LN and more:
                                softplus_log(*ahead)
                            if (d, i) == (1, 1) and not first:
                                residual(b)
                            if i == NI - 1 and first and d == 0:
                                for m in range(DT):
                                    act.activation(d_diag[:, m, :], ident[:, :], ACT.Identity,
                                                   scale=dsk[:, m:m + 1]).then_inc(diag_done, 1)
                    if last:
                        norm_std(act, norm, 0)
                        residual(NB)

                act.wait_ge(one_done, 1)
                softplus_exp(0, 0)
                softplus_log(0, 0)
                act.wait_ge(a_done, 1)
                split_ts(act, ft, NB)
                batches(act, body)

            @block.vector
            def _(dve):
                def softplus_lost(b, d):
                    dve.wait_ge(w_done, b * DT + (d + 1))
                    dve.scalar_tensor_tensor(out=sp1[:, :], in0=sp2[:, :], scalar=-1.0, in1=sp1[:, :],
                                             op0=ALU.add, op1=ALU.subtract).then_inc(round_done, 1)

                def softplus_log(b, d):
                    dve.wait_ge(ln_done, b * DT + (d + 1))
                    dve.tensor_tensor(sp2[:, :], sp2[:, :], sp1[:, :], ALU.subtract).then_inc(log_done, 1)

                def softplus_sum(b, d):
                    dve.wait_ge(log_done, b * DT + (d + 1))
                    dve.scalar_tensor_tensor(out=dt[:, d % 2, :], in0=dtp[:, :], scalar=0.0,
                                             in1=sp2[:, :], op0=ALU.max, op1=ALU.add).then_inc(dt_done, 1)

                def gate_y(b, d):
                    dve.wait_ge(y_done, b * DT + (d + 1))
                    dve.wait_ge(g_in[d % 2], b * (8 * DT) + 16 * (d // 2 + 1))
                    if not isinstance(b, int) or b * DT + d >= 2:
                        dve.wait_ge(op_done, b * DT + (d - 1))
                    dve.tensor_tensor(yg[:, d % 2, :], yp[d % 2][:, :], g[:, d % 2, :], ALU.mult).then_inc(yg_done, 1)

                def own_drive(k):
                    if k == 0:
                        dve.wait_ge(dtu_done, 1)
                    if k in range(0, NI, NI // NQ):
                        dve.wait_ge(bb_in[k * NQ // NI], 16)
                    dve.tensor_tensor(work[:, k % RW, :, :], dtu[:, 0:1, :].broadcast_to([P, 2, L]),
                                      bb[:, 2 * k:2 * k + 2, :], ALU.mult).then_inc(own_done, 1)
                    dve.wait_ge(own_done, k + 1)

                def scan_unit(b, k):
                    dve.wait_ge(decay_done, b * UNITS + (k + 1))
                    if not (isinstance(b, int) and b * UNITS + k < OWN):
                        dve.wait_ge(drive_done, b * UNITS + (k + 1 - OWN))
                    w = work[:, k % RW, :, :].rearrange("p m l -> p (m l)")
                    dve.tensor_tensor_scan(w, decay[:, k % RA, :, :].rearrange("p m l -> p (m l)"), w,
                                           0.0, ALU.mult, ALU.add).then_inc(h_done, 1)

                def read_unit(b, k):
                    if k in range(0, NI, NI // NQ):
                        dve.wait_ge(cc_in[k * NQ // NI], b * 16 + 16)
                    dve.wait_ge(h_done, b * UNITS + (k + 1))
                    n = 2 * (k % NI)
                    w = work[:, k % RW, :, :]
                    dve.tensor_tensor(w, w, cc[:, n:n + 2, :], ALU.mult).then_inc(prod_done, 1)

                def body(b, first, last):
                    for k in range(UNITS):
                        d, i = divmod(k, NI)
                        ahead = (b, d + 1) if d + 1 < DT else (b + 1, 0)
                        more = d + 1 < DT or not last
                        if first and k < OWN:
                            own_drive(k)
                        scan_unit(b, k)
                        if k >= 1 or not first:
                            read_unit(b, k - 1)
                        if i == 2 and not (first and d == 0):
                            gate_y(b, d - 1)
                        if i == AT_EXP and more:
                            softplus_lost(*ahead)
                        if i == AT_SUM and more and d % 2:
                            softplus_log(*ahead)
                        if i == AT_SUM and more:
                            softplus_sum(*ahead)
                    if last:
                        read_unit(b, UNITS - 1)
                        norm_stats(dve, norm, 0)
                        dve.wait_ge(norm.st_done, TB)
                        norm_mean(dve, norm, 0)
                        norm_var(dve, norm, 0)
                        gate_y(b, DT - 1)
                        norm_apply(dve, norm, 0)

                dve.memset(decay[:, :, :, 0:1], 0.0).then_inc(reset_done, 1)
                dve.memset(one[:, :], 1.0).then_inc(one_done, 1)
                dve.wait_ge(reset_done, 1)
                norm_features(dve, ft, NB)
                softplus_lost(0, 0)
                softplus_log(0, 0)
                softplus_sum(0, 0)
                rest_ts(dve, ft, NB)
                batches(dve, body)

            @block.gpsimd
            def _(pool):
                def input_gain(b, d):
                    pool.wait_ge(dt_done, b * DT + (d + 1))
                    pool.wait_ge(u_in[d % 2], b * (8 * DT) + 16 * (d // 2 + 1))
                    pool.tensor_tensor(dtu[:, d % 2, :], dt[:, d % 2, :], u[:, d % 2, :],
                                       ALU.mult).then_inc(dtu_done, 1)

                def softplus_log(b, d):
                    pool.wait_ge(ln_done, b * DT + (d + 1))
                    pool.tensor_tensor(sp2[:, :], sp2[:, :], sp1[:, :], ALU.subtract).then_inc(log_done, 1)

                def body(b, first, last):
                    for k in range(UNITS):
                        d, i = divmod(k, NI)
                        ahead = (b, d + 1) if d + 1 < DT else (b + 1, 0)
                        more = d + 1 < DT or not last
                        if i == 0:
                            pool.wait_ge(dtu_done, b * DT + (d + 1))
                        if k in range(0, NI, NI // NQ):
                            pool.wait_ge(bb_in[k * NQ // NI], b * 16 + 16)
                        if k >= RW or not first:
                            pool.wait_ge(unit_summed, b * UNITS + (k - RW + 1))
                        if first and k < OWN:
                            continue
                        n = 2 * i
                        pool.tensor_tensor(work[:, k % RW, :, :],
                                           dtu[:, d % 2:d % 2 + 1, :].broadcast_to([P, 2, L]),
                                           bb[:, n:n + 2, :], ALU.mult).then_inc(drive_done, 1)
                        if i == AT_SUM and more and d % 2 == 0:
                            softplus_log(*ahead)
                        if i == AT_GAIN and more:
                            input_gain(*ahead)

                input_gain(0, 0)
                batches(pool, body)


def ffn(nc, tensors, norm, xr, x1_out, x1_d, hot_d, rows_d, ident, qw_gu, qw_d, out):
    RQ = 3
    with ExitStack() as c:
        sb, ps, sem = tensors(c)
        wg_hi, wg_lo = sb("wg_hi", [P, KH, 2 * INTER], F32R), sb("wg_lo", [P, KH, 2 * INTER], F32R)
        wd_hi, wd_lo = sb("wd_hi", [P, FT, H], F32R), sb("wd_lo", [P, FT, H], F32R)
        hot_gu, hot_dn = sb("hot_gu", [2 * NG, H], F32R), sb("hot_dn", [2 * NGD, INTER], F32R)
        zeros_gu, zeros_dn = sb("zeros_gu", [NG, 2, PC], F32R), sb("zeros_dn", [NGD, H], F32R)
        scales_gu, scales_dn = sb("scales_gu", [2 * NG, 2, PC], F32R), sb("scales_dn", [2 * NGD, H], F32R)
        q = sb("q", [P, RQ, PC], U32)
        pid, shift = sb("pid2", [P, 1], U32), sb("shift", [P, 1], U32)
        xn = norm.x
        xt_hi, xt_lo = sb("xt_hi2", [P, KH, L], F32R), sb("xt_lo2", [P, KH, L], F32R)
        sg, hf = sb("sg", [P, L]), sb("hf", [P, L])
        h_hi, h_lo = sb("h_hi", [P, 2, L], F32R), sb("h_lo", [P, 2, L], F32R)
        gp = [ps(f"gp{i}", [P, L]) for i in range(2)]
        up = [ps(f"up{i}", [P, L]) for i in range(2)]
        tp = [gp[1], up[1], gp[0], up[0]]
        dp = [ps(f"dp{t}", [P, H]) for t in range(TB)]

        hot_in, rows_dn_in = sem("hot_in"), sem("rows_dn_in")
        rows_in = [sem(f"rows_in{i}") for i in range(2)]
        q_in = [sem(f"q_in{i}") for i in range(RQ)]
        pid_done, shift_done = sem("pid2_done"), sem("shift_done")
        nib_done = sem("nib_done")
        picked = sem("picked")
        sub_done, weight_done = sem("sub_done"), sem("weight_done")
        whi_done, wlo_done = sem("whi_done"), sem("wlo_done")
        xr_in = sem("xr1_in")
        tp_done, hi_done, lo_done = sem("tp2_done"), sem("hi2_done"), sem("lo2_done")
        gate_done, up_done = sem("gate_done"), sem("up_done")
        sg_done, hf_done, hhi_done, hlo_done = sem("sg_done"), sem("hf_done"), sem("hhi_done"), sem("hlo_done")
        dp_done, res_done, out_done = sem("dp_done"), sem("res2_done"), sem("out_done")
        block_done = sem("block_done")

        units = []
        for p in range(PAIRS):
            units += [(False, k, PC * p, P, min(PC, 2 * INTER - PC * p)) for k in range(KH)]
            units += [(True, f, 0, rows(f), H) for f in range(2 * p, min(2 * p + 2, FT))]
        BEFORE = range(0, 5)
        UP = KH + 2

        def after(f, stage):
            if f == 0:
                return (range(5, 7), range(7, 9), range(0))[stage]
            i = 9 + 3 * (f - 1) + stage
            return range(i, min(i + 1, len(units)))

        def zero_scale_banks(i):
            if i < 9:
                return dp[2 * (i % 2)], dp[2 * (i % 2) + 1]
            return gp[1], up[1]

        def pair_units(p):
            return UP * p + KH

        def down_units(f):
            return UP * (f // 2) + KH + f % 2 + 1

        def columns(f):
            width = P if f < FT - 1 else FL
            s = PC * (f // 2) + width * (f % 2 if f < FT - 1 else 0)
            return s, s + (2 * P if f < FT - 1 else FL)

        def weights(of_gu, of_dn, i):
            down, tile, c0, kk, nn = units[i]
            return (of_dn if down else of_gu)[0:kk, tile, c0:c0 + nn]

        def batches(body):
            def run(eng):
                body(0, True, False)
                with eng.Fori(1, NB - 1) as b:
                    body(b, False, False)
                body(NB - 1, False, True)
            return run

        with nc.Block() as block:
            @block.sync
            def _(sp):
                def load_stream(b):
                    sp.dma_start(xr[:, :, :], x1_d[bass.ds(b, 1)].rearrange(
                        "o p t h -> (o p) t h")).then_inc(xr_in, 16)

                def load_rows(p):
                    _, _, c0, _, nn = units[UP * p]
                    src = rows_d[:, 0:NG * 2 * INTER].rearrange("j (g n) -> j g n", g=NG)[:, :, c0:c0 + nn]
                    for dst, j in ((zeros_gu, 0), (scales_gu[0:NG], 1), (scales_gu[NG:2 * NG], 2)):
                        sp.dma_start(dst[:, p % 2, 0:nn].bitcast(F32), src[j]).then_inc(rows_in[p % 2], 16)

                def load_q(i):
                    down, tile, c0, kk, nn = units[i]
                    src = (qw_d if down else qw_gu)[P // QC * tile:P // QC * tile + kk // QC, c0:c0 + nn]
                    sp.dma_start(q[0:kk, i % RQ, 0:nn],
                                 src.unsqueeze(1).broadcast_to([kk // QC, QC, nn])).then_inc(q_in[i % RQ], 16)

                def body(b, first, last):
                    if first:
                        for i in range(RQ, len(units)):
                            if i % UP == 0 and i // UP + 1 < PAIRS:
                                p = i // UP + 1
                                sp.wait_ge(picked, pair_units(p - 2))
                                load_rows(p)
                            if i == 2 * UP:
                                sp.wait_ge(tp_done, KH)
                                norm_load(sp, norm, x1_d, 1)
                            if i == 3 * UP:
                                sp.wait_ge(x1_out, 16 * NB)
                                load_stream(0)
                            sp.wait_ge(whi_done, i - RQ + 1)
                            sp.wait_ge(wlo_done, i - RQ + 1)
                            load_q(i)
                    else:
                        sp.wait_ge(out_done, b * 16 * TB)
                        load_stream(b)
                        if not last:
                            sp.wait_ge(tp_done, b * KH + KH)
                            norm_load(sp, norm, x1_d, b + 1)
                    for t in range(TB):
                        sp.wait_ge(res_done, b * TB + (t + 1))
                        sp.dma_start(out[bass.ds(b, 1), :, t].rearrange("o p h -> (o p) h"),
                                     xr[:, t, :]).then_inc(out_done, 16)

                for i in range(2):
                    sp.dma_start(hot_gu[NG * i:NG * (i + 1), :].bitcast(F32), hot_d[0:NG, 0:H]).then_inc(hot_in, 16)
                load_rows(0)
                for i in range(RQ):
                    load_q(i)
                for i in range(2):
                    sp.dma_start(hot_dn[NGD * i:NGD * (i + 1), :].bitcast(F32),
                                 hot_d[:, H:H + INTER]).then_inc(rows_dn_in, 16)
                src = rows_d[:, NG * 2 * INTER:].rearrange("j (g n) -> j g n", g=NGD)
                for dst, j in ((zeros_dn, 0), (scales_dn[0:NGD], 1), (scales_dn[NGD:2 * NGD], 2)):
                    sp.dma_start(dst[:, :].bitcast(F32), src[j]).then_inc(rows_dn_in, 16)
                load_rows(1)
                batches(body)(sp)
                sp.wait_ge(out_done, 16 * NB * TB)

            @block.tensor
            def _(pe):
                def pick(i):
                    down, tile, c0, kk, nn = units[i]
                    if i == 0:
                        pe.wait_ge(hot_in, 32)
                    if down and tile == 0:
                        pe.wait_ge(rows_dn_in, 16 * 5)
                    if not down and tile == 0:
                        p = i // UP
                        pe.wait_ge(rows_in[p % 2], 48 * (p // 2 + 1))
                    if 2 <= i:
                        pe.wait_ge(weight_done, i - 1 if i < 9 else i)
                    z, s = zero_scale_banks(i)
                    cols = slice(P * tile, P * tile + kk)
                    if down:
                        hot, groups, zero, scale = hot_dn, NGD, zeros_dn, scales_dn
                    else:
                        slot = (i // UP) % 2
                        hot, groups, zero, scale = hot_gu, NG, zeros_gu[:, slot], scales_gu[:, slot]
                    pe.matmul(z[0:kk, 0:nn], hot[0:groups, cols], zero[:, 0:nn], start=True, stop=True)
                    pe.matmul(s[0:kk, 0:nn], hot[:, cols], scale[:, 0:nn], start=True,
                              stop=True).then_inc(picked, 1)

                def transposes(b, ks):
                    for k in ks:
                        for t in range(TB):
                            if k == 0:
                                pe.wait_ge(norm.xn_done, b * TB + (t + 1))
                            last = pe.transpose(tp[k][:, P * t:P * (t + 1)], xn[:, t, P * k:P * (k + 1)],
                                                ident[:, :])
                        last.then_inc(tp_done, 1)

                def down(b, f, first):
                    pe.wait_ge(hhi_done, b * FT + (f + 1))
                    pe.wait_ge(hlo_done, b * FT + (f + 1))
                    if f == 0:
                        if first:
                            pe.wait_ge(weight_done, 9)
                        else:
                            pe.wait_ge(res_done, b * TB)
                    if first:
                        pe.wait_ge(whi_done, down_units(f))
                        pe.wait_ge(wlo_done, down_units(f))
                    r = rows(f)
                    for t in range(TB):
                        s = slice(P * t, P * (t + 1))
                        last_mm = products(pe, dp[t][:, :], h_hi[0:r, f % 2, s], h_lo[0:r, f % 2, s],
                                           wd_hi[0:r, f, :], wd_lo[0:r, f, :],
                                           start=(f == 0), stop=(f == FT - 1))
                        if f == FT - 1 and t < TB - 1:
                            last_mm.then_inc(block_done, 1)
                    last_mm.then_inc(dp_done, 1)

                def body(b, first, last):
                    for f in range(FT):
                        r = rows(f)
                        bank = 0 if first else f % 2
                        if f == 0:
                            pe.wait_ge(hi_done, b * KH + KH)
                            pe.wait_ge(lo_done, b * KH + KH)
                        elif first:
                            pe.wait_ge(sg_done, f)
                            pe.wait_ge(hf_done, f)
                        elif f >= 2:
                            pe.wait_ge(sg_done, b * FT + (f - 1))
                            pe.wait_ge(hf_done, b * FT + (f - 1))
                        if first and f % 2 == 0 and f > 0:
                            pe.wait_ge(whi_done, pair_units(f // 2))
                            pe.wait_ge(wlo_done, pair_units(f // 2))
                        for i, (dst, c0, done) in enumerate(zip((gp[bank], up[bank]), columns(f),
                                                                (gate_done, up_done))):
                            s = slice(c0, c0 + r)
                            for k in range(KH):
                                if first and f == 0 and i == 0:
                                    pe.wait_ge(whi_done, k + 1)
                                    pe.wait_ge(wlo_done, k + 1)
                                last_mm = products(pe, dst[0:r, :], wg_hi[:, k, s], wg_lo[:, k, s],
                                                   xt_hi[:, k, :], xt_lo[:, k, :], start=(k == 0),
                                                   stop=(k == KH - 1))
                            last_mm.then_inc(done, 1)
                            if first:
                                for j in after(f, i):
                                    pick(j)
                        if f == FT - 1 and not last:
                            if first:
                                pe.wait_ge(weight_done, len(units))
                            else:
                                pe.wait_ge(sg_done, b * FT + (FT - 1))
                                pe.wait_ge(hf_done, b * FT + (FT - 1))
                            transposes(b + 1, range(0, 2))
                        if f >= 1:
                            down(b, f - 1, first)
                        if first:
                            for j in after(f, 2):
                                pick(j)
                    if not last:
                        pe.wait_ge(sg_done, b * FT + FT)
                        pe.wait_ge(hf_done, b * FT + FT)
                        transposes(b + 1, range(2, KH))
                    down(b, FT - 1, first)

                transposes(0, range(KH))
                for i in BEFORE:
                    pick(i)
                batches(body)(pe)

            @block.scalar
            def _(act):
                def split_x(b, ks):
                    for k in ks:
                        act.wait_ge(tp_done, b * KH + (k + 1))
                        act.activation(xt_hi[:, k, :], tp[k][:, :], ACT.Copy).then_inc(hi_done, 1)

                def split_w(i):
                    _, _, _, kk, nn = units[i]
                    act.wait_ge(weight_done, i + 1)
                    act.activation(weights(wg_hi, wd_hi, i), q[0:kk, i % RQ, 0:nn].bitcast(F32),
                                   ACT.Copy).then_inc(whi_done, 1)

                def body(b, first, last):
                    for f in range(FT):
                        r = rows(f)
                        bank = 0 if first else f % 2
                        act.wait_ge(gate_done, b * FT + (f + 1))
                        if f >= 1 or not first:
                            act.wait_ge(hf_done, b * FT + f)
                        act.activation(sg[0:r, :], gp[bank][0:r, :], ACT.Silu).then_inc(sg_done, 1)
                        if first:
                            for i in after(f, 0):
                                split_w(i)
                        act.wait_ge(hf_done, b * FT + (f + 1))
                        if f >= 2 or not first:
                            act.wait_ge(dp_done, b * FT + (f - 1))
                        act.activation(h_hi[0:r, f % 2, :], hf[0:r, :], ACT.Copy).then_inc(hhi_done, 1)
                        if first:
                            for i in (*after(f, 1), *after(f, 2)):
                                split_w(i)
                        if f == 5 and not last:
                            norm_std(act, norm, b + 1)
                    if not last:
                        act.wait_ge(up_done, b * FT + FT)
                        split_x(b + 1, range(KH))

                split_x(0, range(KH))
                for i in BEFORE:
                    split_w(i)
                batches(body)(act)

            @block.gpsimd
            def _(pool):
                def rest_w(i):
                    _, _, _, kk, nn = units[i]
                    pool.wait_ge(whi_done, i + 1)
                    pool.tensor_tensor(weights(wg_lo, wd_lo, i), q[0:kk, i % RQ, 0:nn].bitcast(F32),
                                       weights(wg_hi, wd_hi, i).bitcast(F32), ALU.subtract).then_inc(wlo_done, 1)

                def body(b, first, last):
                    for f in range(FT):
                        r = rows(f)
                        if first:
                            for i in after(f, 0):
                                rest_w(i)
                        pool.wait_ge(hhi_done, b * FT + (f + 1))
                        if f >= 2 or not first:
                            pool.wait_ge(dp_done, b * FT + (f - 1))
                        pool.tensor_tensor(h_lo[0:r, f % 2, :], hf[0:r, :], h_hi[0:r, f % 2, :].bitcast(F32),
                                           ALU.subtract).then_inc(hlo_done, 1)
                        if first:
                            for i in (*after(f, 1), *after(f, 2)):
                                rest_w(i)

                pool.iota(pid[:, :], pattern=[[0, 1]], base=0, channel_multiplier=1).then_inc(pid_done, 1)
                for i in BEFORE:
                    rest_w(i)
                batches(body)(pool)

            @block.vector
            def _(dve):
                def rest_x(b):
                    for k in range(KH):
                        dve.wait_ge(hi_done, b * KH + (k + 1))
                        dve.tensor_tensor(xt_lo[:, k, :], tp[k][:, :], xt_hi[:, k, :].bitcast(F32),
                                          ALU.subtract).then_inc(lo_done, 1)

                def nibbles(i):
                    _, _, _, kk, nn = units[i]
                    dve.wait_ge(q_in[i % RQ], 16 * (i // RQ + 1))
                    n = q[0:kk, i % RQ, 0:nn]
                    dve.tensor_scalar(n, n, shift[0:kk, 0:1], 15, ALU.logical_shift_right,
                                      ALU.bitwise_and).then_inc(nib_done, 1)

                def weight(i):
                    _, _, _, kk, nn = units[i]
                    z, s = zero_scale_banks(i)
                    w = q[0:kk, i % RQ, 0:nn].bitcast(F32)
                    dve.wait_ge(nib_done, i + 1)
                    dve.wait_ge(picked, i + 1)
                    dve.tensor_tensor(w, q[0:kk, i % RQ, 0:nn], z[0:kk, 0:nn], ALU.subtract).then_inc(sub_done, 1)
                    dve.wait_ge(sub_done, i + 1)
                    dve.tensor_tensor(w, w, s[0:kk, 0:nn], ALU.mult).then_inc(weight_done, 1)
                    if i + 1 < len(units):
                        nibbles(i + 1)

                def body(b, first, last):
                    for f in range(FT):
                        r = rows(f)
                        bank = 0 if first else f % 2
                        if first:
                            for i in after(f, 0):
                                weight(i)
                        if f == 4 and not last:
                            dve.wait_ge(norm.st_done, (b + 1) * TB + TB)
                        dve.wait_ge(sg_done, b * FT + (f + 1))
                        dve.wait_ge(up_done, b * FT + (f + 1))
                        if f >= 1 or not first:
                            dve.wait_ge(hhi_done, b * FT + f)
                            dve.wait_ge(hlo_done, b * FT + f)
                        dve.tensor_tensor(hf[0:r, :], sg[0:r, :], up[bank][0:r, :],
                                          ALU.mult).then_inc(hf_done, 1)
                        if first:
                            for i in (*after(f, 1), *after(f, 2)):
                                weight(i)
                        if not last:
                            if f == 3:
                                norm_stats(dve, norm, b + 1)
                            if f == 4:
                                norm_mean(dve, norm, b + 1)
                            if f == 5:
                                norm_var(dve, norm, b + 1)
                            if f == 7:
                                norm_apply(dve, norm, b + 1)
                    if not last:
                        rest_x(b + 1)
                    dve.wait_ge(xr_in, b * 16 + 16)
                    for t in range(TB):
                        if t < TB - 1:
                            dve.wait_ge(block_done, b * (TB - 1) + (t + 1))
                        else:
                            dve.wait_ge(dp_done, b * FT + FT)
                        dve.tensor_tensor(xr[:, t, :], dp[t][:, :], xr[:, t, :], ALU.add).then_inc(res_done, 1)

                dve.wait_ge(pid_done, 1)
                dve.tensor_scalar(shift[:, :], pid[:, :], QC - 1, 2, ALU.bitwise_and,
                                  ALU.logical_shift_left).then_inc(shift_done, 1)
                dve.wait_ge(shift_done, 1)
                rest_x(0)
                nibbles(0)
                for i in BEFORE:
                    weight(i)
                batches(body)(dve)


def kernel(**inputs):
    import numpy as np
    import concourse.bacc as bacc
    from concourse.bass_utils import run_bass_kernel_spmd as run

    get = lambda n: np.asarray(inputs[n])
    group_mean = np.zeros((SF, P), np.float32)
    for f0, f1 in ((0, R), (R, R + NS), (R + NS, SF)):
        group_mean[f0:f1, f0:f1] = 1.0 / (f1 - f0)
    cols = np.concatenate([np.arange(half + 2 * P * p, half + min(2 * P * (p + 1), INTER))
                           for p in range(PAIRS) for half in (0, INTER)])
    lay = {
        "x": get("L0_attn_hidden_states").reshape(NB, TB, P, H).transpose(0, 2, 1, 3),
        "w_in": get("L0_attn_W_in").reshape(2, DT, P, KH, P).transpose(4, 1, 0, 3, 2).reshape(P, DT, 2 * KH * P),
        "conv_w": get("L0_attn_conv_w").reshape(DT, P, TAPS).transpose(1, 0, 2),
        "conv_b": get("L0_attn_conv_b").reshape(DT, P).T,
        "w_x": get("L0_attn_W_x").T.reshape(DT, P, SF).transpose(1, 0, 2),
        "w_dt": np.concatenate([get("L0_attn_W_dt").T, get("L0_attn_b_dt")[None]], 0),
        "a_log": get("L0_attn_A_log").reshape(DT, P, NS).transpose(1, 0, 2),
        "d_skip": get("L0_attn_D").reshape(DT, P).T,
        "group_mean": group_mean,
        "w_out": get("L0_attn_W_out").T.reshape(DT, P, H).transpose(1, 0, 2),
        "qw_gu": get("L0_ffn_qweight_gu")[:, cols],
        "qw_d": get("L0_ffn_qweight_down"),
        "zeros": np.concatenate([get("L0_ffn_qzeros_gu")[:, cols[::QC] // QC].reshape(-1, P // QC),
                                 get("L0_ffn_qzeros_down").reshape(-1, P // QC)], 0),
        "scales": np.concatenate([get("L0_ffn_scales_gu")[:, cols].reshape(-1, P),
                                  get("L0_ffn_scales_down").reshape(-1, P)], 0),
        "g_idx": np.concatenate([get("L0_ffn_g_idx_gu"), get("L0_ffn_g_idx_down")])[None],
    }
    nc = bacc.Bacc("TRN2", target_bir_lowering=False, num_devices=1)
    arrays, args = {}, []
    for name, a in lay.items():
        a = np.ascontiguousarray(a)
        arrays[name] = a
        args.append(nc.dram_tensor(name, a.shape, mybir.dt.from_np(a.dtype), kind="ExternalInput").ap())
    args.append(nc.dram_tensor("out", (NB, P, TB, H), F32, kind="ExternalOutput").ap())
    build(nc, *args)
    r = run(nc, [arrays], core_ids=[0])
    return r.results[0]["out"].transpose(0, 2, 1, 3).reshape(NB, L, H)
```
